# Optimizing a Trainium2 kernel written in Bass

```python
import numpy as np
import jax
import jax.numpy as jnp

def _softmax(x, axis=-1):
    return jax.nn.softmax(x, axis=axis)

def _gelu(x):
    return jax.nn.gelu(x, approximate=True)

def _silu(x):
    return jax.nn.silu(x)

def _sigmoid(x):
    return jax.nn.sigmoid(x)

def _layernorm(x, axis=-1, eps=1e-05):
    m = jnp.mean(x, axis=axis, keepdims=True)
    v = jnp.var(x, axis=axis, keepdims=True)
    return (x - m) / jnp.sqrt(v + eps)

def _scatter_add(tgt, idx, src, axis=0):
    return tgt.at[idx].add(src)

def _segment_sum(src, seg, n):
    return jax.ops.segment_sum(src, seg, n)
kernel_name = 'mk_lm_tower_d1_tok_ids768_r4_f76e00'

def setup_inputs(seed: int=0):
    np.random.seed(seed)
    _w = jnp.asarray

    def _rec_inputs():
        import jax
        import jax.numpy as jnp
        _rk = jax.random.key(seed)
        x = jax.random.randint(jax.random.fold_in(_rk, 1), (16, 512), 0, 8000, jnp.int32)
        itok_BS_0_511 = jax.random.randint(jax.random.fold_in(_rk, 21), (16, 512), 0, 128, jnp.int32)
        return (x, itok_BS_0_511)
    x, itok_BS_0_511 = _rec_inputs()

    def _L0_tok_setup():
        import jax, jax.numpy as jnp
        import numpy as np
        V, NV, NF, NG = (8000, 128, 16, 32)
        B, L, H, D = (16, 2048, 64, 192)
        IN_DIM = 6 + NF + 4 + 11
        SPECIAL_TOKEN_IDS = (0, 1, 2)
        LN_EPS = 1e-05

        def _forward(token_ids, var_ids, token_has_int, token_signed_norm, token_log_norm, token_is_zero, token_is_one, token_is_pow2, var_family_onehot, var_outer_norm, var_inner_norm, var_has_outer, var_has_inner, var_family_id, var_group_id, ln_gamma, ln_beta, W1, b1, W2, b2, scale):
            bsz, seq_len = token_ids.shape
            dt = token_log_norm.dtype
            has_int = token_has_int[token_ids]
            tok_signed = token_signed_norm[token_ids]
            tok_log = token_log_norm[token_ids]
            tok_zero = token_is_zero[token_ids]
            tok_one = token_is_one[token_ids]
            tok_pow2 = token_is_pow2[token_ids]
            fam_oh = var_family_onehot[var_ids]
            fam_id = var_family_id[var_ids]
            outer = var_outer_norm[var_ids]
            inner = var_inner_norm[var_ids]
            has_outer = var_has_outer[var_ids]
            has_inner = var_has_inner[var_ids]
            gid = var_group_id[var_ids]
            valid = has_int > 0.0
            for s in SPECIAL_TOKEN_IDS:
                valid = valid & (token_ids != s)
            vf = valid.astype(dt)
            denom = float(max(seq_len - 1, 1))
            pos_norm = jnp.broadcast_to(jnp.arange(seq_len, dtype=dt)[None, :] / denom, (bsz, seq_len))
            tok_log_v = tok_log * vf
            prev_count = jnp.cumsum(vf, axis=1) - vf
            prev_logsum = jnp.cumsum(tok_log_v, axis=1) - tok_log_v
            prev_count_n = prev_count / denom
            prev_logsum_n = prev_logsum / denom
            prev_tok_log = jnp.pad(tok_log[:, :-1], ((0, 0), (1, 0)))
            prev_tok_signed = jnp.pad(tok_signed[:, :-1], ((0, 0), (1, 0)))
            fam_valid = fam_oh * vf[..., None]
            fam_logv = fam_oh * tok_log_v[..., None]
            fam_pc = jnp.cumsum(fam_valid, axis=1) - fam_valid
            fam_pl = jnp.cumsum(fam_logv, axis=1) - fam_logv
            fidx = fam_id[..., None].astype(jnp.int32)
            psf_c = jnp.take_along_axis(fam_pc, fidx, axis=-1)[..., 0]
            psf_l = jnp.take_along_axis(fam_pl, fidx, axis=-1)[..., 0]
            cnt_floor = jnp.maximum(prev_count, 1.0)
            psf_c_n = psf_c / denom
            psf_l_n = psf_l / denom
            psf_ratio = psf_c / cnt_floor
            g_oh = jax.nn.one_hot(jnp.maximum(gid, 0), NG, dtype=dt)
            vg = (gid > 0).astype(dt)
            g_valid = g_oh * (vf * vg)[..., None]
            g_logv = g_oh * (tok_log_v * vg)[..., None]
            g_pc = jnp.cumsum(g_valid, axis=1) - g_valid
            g_pl = jnp.cumsum(g_logv, axis=1) - g_logv
            gidx = gid[..., None].astype(jnp.int32)
            psg_c = jnp.take_along_axis(g_pc, gidx, axis=-1)[..., 0]
            psg_l = jnp.take_along_axis(g_pl, gidx, axis=-1)[..., 0]
            psg_c = jnp.where(gid > 0, psg_c, 0.0)
            psg_l = jnp.where(gid > 0, psg_l, 0.0)
            psg_c_n = psg_c / denom
            psg_l_n = psg_l / denom
            psg_ratio = psg_c / cnt_floor
            static_token = jnp.stack([has_int, tok_signed, tok_log, tok_zero, tok_one, tok_pow2], axis=-1)
            static_var = jnp.concatenate([fam_oh, outer[..., None], inner[..., None], has_outer[..., None], has_inner[..., None]], axis=-1)
            dynamic = jnp.stack([pos_norm, prev_count_n, prev_logsum_n, psf_c_n, psf_l_n, psf_ratio, psg_c_n, psg_l_n, psg_ratio, prev_tok_log, prev_tok_signed], axis=-1)
            feat = jnp.concatenate([static_token, static_var, dynamic], axis=-1)
            mu = jnp.mean(feat, axis=-1, keepdims=True)
            var = jnp.mean(jnp.square(feat - mu), axis=-1, keepdims=True)
            x = (feat - mu) * jax.lax.rsqrt(var + LN_EPS) * ln_gamma + ln_beta
            h = jax.nn.gelu(x @ W1 + b1, approximate=False)
            return scale * (h @ W2 + b2)
        key = jax.random.key(seed)
        ks = jax.random.split(key, 18)
        token_ids = jax.random.randint(ks[0], (B, L), 0, V, dtype=jnp.int32)
        var_ids = jax.random.randint(ks[1], (B, L), 0, NV, dtype=jnp.int32)
        token_has_int = (jax.random.uniform(ks[2], (V,)) > 0.3).astype(jnp.float32)
        token_signed_norm = jax.random.normal(ks[3], (V,), dtype=jnp.float32)
        token_log_norm = jax.random.normal(ks[4], (V,), dtype=jnp.float32)
        token_is_zero = (jax.random.uniform(ks[5], (V,)) > 0.9).astype(jnp.float32)
        token_is_one = (jax.random.uniform(ks[6], (V,)) > 0.9).astype(jnp.float32)
        token_is_pow2 = (jax.random.uniform(ks[7], (V,)) > 0.8).astype(jnp.float32)
        var_family_id = jax.random.randint(ks[8], (NV,), 0, NF, dtype=jnp.int32)
        var_family_onehot = jax.nn.one_hot(var_family_id, NF, dtype=jnp.float32)
        var_outer_norm = jax.random.uniform(ks[9], (NV,), dtype=jnp.float32)
        var_inner_norm = jax.random.uniform(ks[10], (NV,), dtype=jnp.float32)
        var_has_outer = (jax.random.uniform(ks[11], (NV,)) > 0.5).astype(jnp.float32)
        var_has_inner = (jax.random.uniform(ks[12], (NV,)) > 0.5).astype(jnp.float32)
        var_group_id = jax.random.randint(ks[13], (NV,), 0, NG, dtype=jnp.int32)
        ln_gamma = jnp.ones((IN_DIM,), jnp.float32)
        ln_beta = jnp.zeros((IN_DIM,), jnp.float32)
        W1 = jax.random.normal(ks[14], (IN_DIM, H), dtype=jnp.float32) / np.sqrt(IN_DIM).astype(np.float32)
        b1 = jnp.zeros((H,), jnp.float32)
        W2 = jax.random.normal(ks[15], (H, D), dtype=jnp.float32) / np.sqrt(H).astype(np.float32)
        b2 = jnp.zeros((D,), jnp.float32)
        scale = jnp.asarray(0.1, jnp.float32)
        return dict(token_ids=token_ids, var_ids=var_ids, token_has_int=token_has_int, token_signed_norm=token_signed_norm, token_log_norm=token_log_norm, token_is_zero=token_is_zero, token_is_one=token_is_one, token_is_pow2=token_is_pow2, var_family_onehot=var_family_onehot, var_outer_norm=var_outer_norm, var_inner_norm=var_inner_norm, var_has_outer=var_has_outer, var_has_inner=var_has_inner, var_family_id=var_family_id, var_group_id=var_group_id, ln_gamma=ln_gamma, ln_beta=ln_beta, W1=W1, b1=b1, W2=W2, b2=b2, scale=scale)
    _L0_tok_all = _L0_tok_setup()
    _L0_tok_in = {k: v for k, v in _L0_tok_all.items() if k in ('token_has_int', 'token_signed_norm', 'token_log_norm', 'token_is_zero', 'token_is_one', 'token_is_pow2', 'var_family_onehot', 'var_outer_norm', 'var_inner_norm', 'var_has_outer', 'var_has_inner', 'var_family_id', 'var_group_id', 'ln_gamma', 'ln_beta', 'W1', 'b1', 'W2', 'b2', 'scale')}
    del _L0_tok_all

    def _L0_attn_setup():
        import jax, jax.numpy as jnp
        import numpy as np
        from jax import lax
        B_SZ, L, D, N, R = (1, 1024, 192, 16, 48)

        def _soft_clamp(x, lo=0.0001, hi=10.0):
            center = (hi + lo) / 2.0
            half_range = (hi - lo) / 2.0
            return center + half_range * jnp.tanh((x - center) / half_range)
        key = jax.random.key(seed)
        ks = jax.random.split(key, 6)
        x = jax.random.normal(ks[0], (B_SZ, L, D), jnp.float32)
        A_log = jnp.log(jnp.broadcast_to(jnp.arange(1, N + 1, dtype=jnp.float32), (D, N)))
        D_param = jnp.ones((D,), jnp.float32)
        W_bc = jax.random.normal(ks[1], (D, 2 * N), jnp.float32) / np.sqrt(D).astype(np.float32)
        W_dt = jax.random.normal(ks[2], (D, R), jnp.float32) / np.sqrt(D).astype(np.float32)
        W_dtp = jax.random.normal(ks[3], (R, D), jnp.float32) / np.sqrt(R).astype(np.float32)
        dt = jax.random.uniform(ks[4], (D,), jnp.float32, 0.001, 0.1)
        dt = jnp.clip(dt, 0.0001)
        b_dt = dt + jnp.log(-jnp.expm1(-dt))
        rms_scale = jnp.ones((D,), jnp.float32)
        return {'x': x, 'A_log': A_log, 'D_param': D_param, 'W_bc': W_bc, 'W_dt': W_dt, 'W_dtp': W_dtp, 'b_dt': b_dt, 'rms_scale': rms_scale}
    _L0_attn_all = _L0_attn_setup()
    _L0_attn_in = {k: v for k, v in _L0_attn_all.items() if k in ('A_log', 'D_param', 'W_bc', 'W_dt', 'W_dtp', 'b_dt', 'rms_scale')}
    del _L0_attn_all

    def _L0_ffn_setup():
        import jax, jax.numpy as jnp
        import numpy as np
        QN, QP = (-8, 7)

        def round_pass(x):
            return x + jax.lax.stop_gradient(jnp.round(x) - x)

        def _quant_act(x, alpha_a):
            a = alpha_a.mean()
            return round_pass(jnp.clip(x / a, QN, QP))

        def _quant_w(w, alpha_w):
            return round_pass(jnp.clip(w / alpha_w[:, None], QN, QP))
        key = jax.random.key(seed)
        ks = jax.random.split(key, 9)
        B, S, D, H = (16, 256, 192, 768)

        def unif(k, shape):
            return jax.random.uniform(k, shape, jnp.float32, 0.02, 0.1)
        return {'x0': jax.random.normal(ks[0], (B, S, D), jnp.float32), 'w1': jax.random.normal(ks[1], (H, D), jnp.float32) * 0.02, 'b1': jax.random.normal(ks[2], (H,), jnp.float32) * 0.02, 'alpha_w1': unif(ks[3], (H,)), 'alpha_a1': unif(ks[4], (D,)), 'w2': jax.random.normal(ks[5], (D, H), jnp.float32) * 0.02, 'b2': jax.random.normal(ks[6], (D,), jnp.float32) * 0.02, 'alpha_w2': unif(ks[7], (D,)), 'alpha_a2': unif(ks[8], (H,))}
    _L0_ffn_all = _L0_ffn_setup()
    _L0_ffn_in = {k: v for k, v in _L0_ffn_all.items() if k in ('w1', 'b1', 'alpha_w1', 'alpha_a1', 'w2', 'b2', 'alpha_w2', 'alpha_a2')}
    del _L0_ffn_all
    return {'x': x, 'itok_BS_0_511': itok_BS_0_511, 'L0_tok_token_has_int': _L0_tok_in['token_has_int'], 'L0_tok_token_signed_norm': _L0_tok_in['token_signed_norm'], 'L0_tok_token_log_norm': _L0_tok_in['token_log_norm'], 'L0_tok_token_is_zero': _L0_tok_in['token_is_zero'], 'L0_tok_token_is_one': _L0_tok_in['token_is_one'], 'L0_tok_token_is_pow2': _L0_tok_in['token_is_pow2'], 'L0_tok_var_family_onehot': _L0_tok_in['var_family_onehot'], 'L0_tok_var_outer_norm': _L0_tok_in['var_outer_norm'], 'L0_tok_var_inner_norm': _L0_tok_in['var_inner_norm'], 'L0_tok_var_has_outer': _L0_tok_in['var_has_outer'], 'L0_tok_var_has_inner': _L0_tok_in['var_has_inner'], 'L0_tok_var_family_id': _L0_tok_in['var_family_id'], 'L0_tok_var_group_id': _L0_tok_in['var_group_id'], 'L0_tok_ln_gamma': _L0_tok_in['ln_gamma'], 'L0_tok_ln_beta': _L0_tok_in['ln_beta'], 'L0_tok_W1': _L0_tok_in['W1'], 'L0_tok_b1': _L0_tok_in['b1'], 'L0_tok_W2': _L0_tok_in['W2'], 'L0_tok_b2': _L0_tok_in['b2'], 'L0_tok_scale': _L0_tok_in['scale'], 'L0_attn_A_log': _L0_attn_in['A_log'], 'L0_attn_D_param': _L0_attn_in['D_param'], 'L0_attn_W_bc': _L0_attn_in['W_bc'], 'L0_attn_W_dt': _L0_attn_in['W_dt'], 'L0_attn_W_dtp': _L0_attn_in['W_dtp'], 'L0_attn_b_dt': _L0_attn_in['b_dt'], 'L0_attn_rms_scale': _L0_attn_in['rms_scale'], 'L0_ffn_w1': _L0_ffn_in['w1'], 'L0_ffn_b1': _L0_ffn_in['b1'], 'L0_ffn_alpha_w1': _L0_ffn_in['alpha_w1'], 'L0_ffn_alpha_a1': _L0_ffn_in['alpha_a1'], 'L0_ffn_w2': _L0_ffn_in['w2'], 'L0_ffn_b2': _L0_ffn_in['b2'], 'L0_ffn_alpha_w2': _L0_ffn_in['alpha_w2'], 'L0_ffn_alpha_a2': _L0_ffn_in['alpha_a2']}

def reference(x, itok_BS_0_511, L0_tok_token_has_int, L0_tok_token_signed_norm, L0_tok_token_log_norm, L0_tok_token_is_zero, L0_tok_token_is_one, L0_tok_token_is_pow2, L0_tok_var_family_onehot, L0_tok_var_outer_norm, L0_tok_var_inner_norm, L0_tok_var_has_outer, L0_tok_var_has_inner, L0_tok_var_family_id, L0_tok_var_group_id, L0_tok_ln_gamma, L0_tok_ln_beta, L0_tok_W1, L0_tok_b1, L0_tok_W2, L0_tok_b2, L0_tok_scale, L0_attn_A_log, L0_attn_D_param, L0_attn_W_bc, L0_attn_W_dt, L0_attn_W_dtp, L0_attn_b_dt, L0_attn_rms_scale, L0_ffn_w1, L0_ffn_b1, L0_ffn_alpha_w1, L0_ffn_alpha_a1, L0_ffn_w2, L0_ffn_b2, L0_ffn_alpha_w2, L0_ffn_alpha_a2):
    import jax
    import jax.numpy as jnp

    def _L0_tok_ref(token_ids, var_ids, token_has_int, token_signed_norm, token_log_norm, token_is_zero, token_is_one, token_is_pow2, var_family_onehot, var_outer_norm, var_inner_norm, var_has_outer, var_has_inner, var_family_id, var_group_id, ln_gamma, ln_beta, W1, b1, W2, b2, scale):
        import jax, jax.numpy as jnp
        import numpy as np
        V, NV, NF, NG = (8000, 128, 16, 32)
        B, L, H, D = (16, 2048, 64, 192)
        IN_DIM = 6 + NF + 4 + 11
        SPECIAL_TOKEN_IDS = (0, 1, 2)
        LN_EPS = 1e-05

        def _forward(token_ids, var_ids, token_has_int, token_signed_norm, token_log_norm, token_is_zero, token_is_one, token_is_pow2, var_family_onehot, var_outer_norm, var_inner_norm, var_has_outer, var_has_inner, var_family_id, var_group_id, ln_gamma, ln_beta, W1, b1, W2, b2, scale):
            bsz, seq_len = token_ids.shape
            dt = token_log_norm.dtype
            has_int = token_has_int[token_ids]
            tok_signed = token_signed_norm[token_ids]
            tok_log = token_log_norm[token_ids]
            tok_zero = token_is_zero[token_ids]
            tok_one = token_is_one[token_ids]
            tok_pow2 = token_is_pow2[token_ids]
            fam_oh = var_family_onehot[var_ids]
            fam_id = var_family_id[var_ids]
            outer = var_outer_norm[var_ids]
            inner = var_inner_norm[var_ids]
            has_outer = var_has_outer[var_ids]
            has_inner = var_has_inner[var_ids]
            gid = var_group_id[var_ids]
            valid = has_int > 0.0
            for s in SPECIAL_TOKEN_IDS:
                valid = valid & (token_ids != s)
            vf = valid.astype(dt)
            denom = float(max(seq_len - 1, 1))
            pos_norm = jnp.broadcast_to(jnp.arange(seq_len, dtype=dt)[None, :] / denom, (bsz, seq_len))
            tok_log_v = tok_log * vf
            prev_count = jnp.cumsum(vf, axis=1) - vf
            prev_logsum = jnp.cumsum(tok_log_v, axis=1) - tok_log_v
            prev_count_n = prev_count / denom
            prev_logsum_n = prev_logsum / denom
            prev_tok_log = jnp.pad(tok_log[:, :-1], ((0, 0), (1, 0)))
            prev_tok_signed = jnp.pad(tok_signed[:, :-1], ((0, 0), (1, 0)))
            fam_valid = fam_oh * vf[..., None]
            fam_logv = fam_oh * tok_log_v[..., None]
            fam_pc = jnp.cumsum(fam_valid, axis=1) - fam_valid
            fam_pl = jnp.cumsum(fam_logv, axis=1) - fam_logv
            fidx = fam_id[..., None].astype(jnp.int32)
            psf_c = jnp.take_along_axis(fam_pc, fidx, axis=-1)[..., 0]
            psf_l = jnp.take_along_axis(fam_pl, fidx, axis=-1)[..., 0]
            cnt_floor = jnp.maximum(prev_count, 1.0)
            psf_c_n = psf_c / denom
            psf_l_n = psf_l / denom
            psf_ratio = psf_c / cnt_floor
            g_oh = jax.nn.one_hot(jnp.maximum(gid, 0), NG, dtype=dt)
            vg = (gid > 0).astype(dt)
            g_valid = g_oh * (vf * vg)[..., None]
            g_logv = g_oh * (tok_log_v * vg)[..., None]
            g_pc = jnp.cumsum(g_valid, axis=1) - g_valid
            g_pl = jnp.cumsum(g_logv, axis=1) - g_logv
            gidx = gid[..., None].astype(jnp.int32)
            psg_c = jnp.take_along_axis(g_pc, gidx, axis=-1)[..., 0]
            psg_l = jnp.take_along_axis(g_pl, gidx, axis=-1)[..., 0]
            psg_c = jnp.where(gid > 0, psg_c, 0.0)
            psg_l = jnp.where(gid > 0, psg_l, 0.0)
            psg_c_n = psg_c / denom
            psg_l_n = psg_l / denom
            psg_ratio = psg_c / cnt_floor
            static_token = jnp.stack([has_int, tok_signed, tok_log, tok_zero, tok_one, tok_pow2], axis=-1)
            static_var = jnp.concatenate([fam_oh, outer[..., None], inner[..., None], has_outer[..., None], has_inner[..., None]], axis=-1)
            dynamic = jnp.stack([pos_norm, prev_count_n, prev_logsum_n, psf_c_n, psf_l_n, psf_ratio, psg_c_n, psg_l_n, psg_ratio, prev_tok_log, prev_tok_signed], axis=-1)
            feat = jnp.concatenate([static_token, static_var, dynamic], axis=-1)
            mu = jnp.mean(feat, axis=-1, keepdims=True)
            var = jnp.mean(jnp.square(feat - mu), axis=-1, keepdims=True)
            x = (feat - mu) * jax.lax.rsqrt(var + LN_EPS) * ln_gamma + ln_beta
            h = jax.nn.gelu(x @ W1 + b1, approximate=False)
            return scale * (h @ W2 + b2)
        return _forward(token_ids, var_ids, token_has_int, token_signed_norm, token_log_norm, token_is_zero, token_is_one, token_is_pow2, var_family_onehot, var_outer_norm, var_inner_norm, var_has_outer, var_has_inner, var_family_id, var_group_id, ln_gamma, ln_beta, W1, b1, W2, b2, scale)

    def _L0_attn_ref(x, A_log, D_param, W_bc, W_dt, W_dtp, b_dt, rms_scale):
        import jax, jax.numpy as jnp
        import numpy as np
        from jax import lax
        B_SZ, L, D, N, R = (1, 1024, 192, 16, 48)

        def _soft_clamp(x, lo=0.0001, hi=10.0):
            center = (hi + lo) / 2.0
            half_range = (hi - lo) / 2.0
            return center + half_range * jnp.tanh((x - center) / half_range)
        n = A_log.shape[1]
        A = -jnp.exp(A_log)
        bc = x @ W_bc
        B_sel, C_sel = (bc[..., :n], bc[..., n:])
        delta = jax.nn.softplus(x @ W_dt @ W_dtp + b_dt)
        delta = delta * lax.rsqrt(jnp.mean(delta * delta, axis=-1, keepdims=True) + 1e-06) * rms_scale
        delta = _soft_clamp(delta, 0.0001, 10.0)
        dE = delta[..., None]
        half = 0.5 * dE * A
        denom = 1.0 - half
        A_bar = (1.0 + half) / denom
        B_bar = jnp.sqrt(dE) * B_sel[:, :, None, :] / denom
        x_prev = jnp.concatenate([jnp.zeros_like(x[:, :1]), x[:, :-1]], axis=1)
        x_in = 0.5 * (x + x_prev)
        Bx = B_bar * x_in[..., None]

        def op(left, right):
            a_l, b_l = left
            a_r, b_r = right
            return (a_r * a_l, a_r * b_l + b_r)
        _, all_h = lax.associative_scan(op, (A_bar, Bx), axis=1)
        y = jnp.sum(C_sel[:, :, None, :] * all_h, axis=-1)
        return y + D_param * x

    def _L0_ffn_ref(x0, w1, b1, alpha_w1, alpha_a1, w2, b2, alpha_w2, alpha_a2):
        import jax, jax.numpy as jnp
        import numpy as np
        QN, QP = (-8, 7)

        def round_pass(x):
            return x + jax.lax.stop_gradient(jnp.round(x) - x)

        def _quant_act(x, alpha_a):
            a = alpha_a.mean()
            return round_pass(jnp.clip(x / a, QN, QP))

        def _quant_w(w, alpha_w):
            return round_pass(jnp.clip(w / alpha_w[:, None], QN, QP))
        xq = _quant_act(x0, alpha_a1)
        wq1 = _quant_w(w1, alpha_w1)
        x1 = jnp.einsum('bsd,hd->bsh', xq, wq1)
        x1 = x1 * alpha_w1 * alpha_a1.mean() + b1
        x1 = jax.nn.gelu(x1, approximate=False)
        x1 = jnp.clip(x1, -10.0, 10.0)
        hq = _quant_act(x1, alpha_a2)
        wq2 = _quant_w(w2, alpha_w2)
        x2 = jnp.einsum('bsh,dh->bsd', hq, wq2)
        x2 = x2 * alpha_w2 * alpha_a2.mean() + b2
        return x2
    h = _L0_tok_ref(x, itok_BS_0_511, L0_tok_token_has_int, L0_tok_token_signed_norm, L0_tok_token_log_norm, L0_tok_token_is_zero, L0_tok_token_is_one, L0_tok_token_is_pow2, L0_tok_var_family_onehot, L0_tok_var_outer_norm, L0_tok_var_inner_norm, L0_tok_var_has_outer, L0_tok_var_has_inner, L0_tok_var_family_id, L0_tok_var_group_id, L0_tok_ln_gamma, L0_tok_ln_beta, L0_tok_W1, L0_tok_b1, L0_tok_W2, L0_tok_b2, L0_tok_scale)
    h = h + _L0_attn_ref(_layernorm(h, axis=-1), L0_attn_A_log, L0_attn_D_param, L0_attn_W_bc, L0_attn_W_dt, L0_attn_W_dtp, L0_attn_b_dt, L0_attn_rms_scale)
    h = h + _L0_ffn_ref(_layernorm(h, axis=-1), L0_ffn_w1, L0_ffn_b1, L0_ffn_alpha_w1, L0_ffn_alpha_a1, L0_ffn_w2, L0_ffn_b2, L0_ffn_alpha_w2, L0_ffn_alpha_a2)
    return h

_drawn_inputs = setup_inputs


def setup_inputs(seed=0):
    import zlib

    import numpy as np

    out = dict(_drawn_inputs(seed))
    spreads = {'L0_tok_ln_gamma': (1.0, 0.2),
     'L0_tok_ln_beta': (0.0, 0.1),
     'L0_tok_b1': (0.0, 0.1),
     'L0_tok_b2': (0.0, 0.1),
     'L0_attn_D_param': (1.0, 0.2),
     'L0_attn_rms_scale': (1.0, 0.6)}
    factors = {'L0_ffn_b1': 60.072,
     'L0_ffn_alpha_w1': 30.336,
     'L0_ffn_b2': 3.754,
     'L0_ffn_alpha_w2': 32.456,
     'L0_ffn_alpha_a2': 200.0,
     'L0_ffn_w1': 8.0,
     'L0_ffn_w2': 8.0}
    for name, (base, spread) in spreads.items():
        noise = np.random.default_rng([zlib.crc32(name.encode()), seed]).standard_normal(out[name].shape)
        drawn = base * np.exp(spread * noise) if base else spread * noise
        out[name] = jnp.asarray(drawn.astype(out[name].dtype))
    for name, factor in factors.items():
        out[name] = (out[name] * factor).astype(out[name].dtype)
    return out
```

```python
import concourse.bass as bass
from concourse import mybir
from contextlib import ExitStack
import math


def lm_tower_kernel(
    nc: bass.Bass,
    tok_ids: bass.AP,
    var_ids: bass.AP,
    tok_table: bass.AP,
    fam_onehot: bass.AP,
    var_cols: bass.AP,
    var_int: bass.AP,
    ln_gamma: bass.AP,
    ln_beta: bass.AP,
    W1: bass.AP,
    b1: bass.AP,
    W2: bass.AP,
    b2: bass.AP,
    tok_scale: bass.AP,
    A_log_lo: bass.AP,
    A_log_hi: bass.AP,
    D_param: bass.AP,
    W_bc: bass.AP,
    W_dt: bass.AP,
    W_dtp: bass.AP,
    b_dt: bass.AP,
    rms_scale: bass.AP,
    ffn_w1T: bass.AP,
    ffn_b1: bass.AP,
    alpha_w1_col: bass.AP,
    alpha_w1_row: bass.AP,
    alpha_a1: bass.AP,
    ffn_w2T: bass.AP,
    ffn_b2: bass.AP,
    alpha_w2: bass.AP,
    alpha_a2: bass.AP,
    out: bass.AP,
):
    f32, bf16, i32 = mybir.dt.float32, mybir.dt.bfloat16, mybir.dt.int32
    ALU = mybir.AluOpType
    ACT = mybir.ActivationFunctionType
    AXX = mybir.AxisListType.X

    P = 128
    BATCH, S = var_ids.shape
    JB = S // P
    NV, NF = fam_onehot.shape
    NG = 32
    IN, H = W1.shape
    D = W2.shape[1]
    DH = D - P
    N = A_log_lo.shape[1]
    R = W_dt.shape[1]
    FF = ffn_w1T.shape[1]
    FC = FF // P
    NT = 6
    VW = NF + 4
    SEL = NF + NG
    CW = 2 + 2 * NF + 2 * NG
    GROUPS = N // 2
    TG = 3
    TILES = GROUPS * TG
    WR, AR, ER = 4, 4, 3
    ACC = JB * (1 + N)
    LO, HI = 0.0001, 10.0
    MID, HALF = (HI + LO) / 2.0, (HI - LO) / 2.0
    MAGIC = 12582912.0
    QN, QP = -8.0, 7.0
    INV_LEN = 1.0 / float(S - 1)
    LN_EPS, RMS_EPS = 1e-5, 1e-6

    ctx = ExitStack()
    with ctx:
        def sb(name, shape, dt=f32):
            return ctx.enter_context(nc.sbuf_tensor(name, shape, dt))

        def sem(name):
            return ctx.enter_context(nc.semaphore(name))

        ident = sb("ident", [P, P])
        ident_bf = sb("ident_bf", [P, P], bf16)
        bidiag = sb("bidiag", [P, P + 1])
        before = sb("before", [P, P])
        ones = sb("ones", [P, P])
        shift = sb("shift", [P, P])
        edge = sb("edge", [P, P])
        avg = sb("avg", [P, P])
        avg_edge = sb("avg_edge", [P, P])
        row_id = sb("row_id", [P, 1])
        col_id = sb("col_id", [P, NG])
        minus_half = sb("minus_half", [P, JB])
        tok_sb = sb("tok_sb", [P, BATCH * JB], i32)
        var_table = sb("var_table", [NV, VW + SEL])
        vint = sb("vint", [NV, 2], i32)
        vintf = sb("vintf", [NV, 2])
        vgrp = sb("vgrp", [NV, 1])
        gamma_sb = sb("gamma_sb", [IN, 1])
        beta_sb = sb("beta_sb", [IN, 1])
        w1_sb = sb("w1_sb", [IN, H])
        w1g = sb("w1g", [IN, H])
        b1_sb = sb("b1_sb", [H, 1])
        bias1 = sb("bias1", [H, 1])
        w2_sb = sb("w2_sb", [H + 1, D])
        scale_sb = sb("scale_sb", [H + 1, 1])
        abias_lo = sb("abias_lo", [P, N])
        abias_hi = sb("abias_hi", [P, N // 2])
        d_row = sb("d_row", [P, D])
        rms_row = sb("rms_row", [P, D])
        wbc_lo = sb("wbc_lo", [P, 2 * N])
        wbc_hi = sb("wbc_hi", [DH, 2 * N])
        wdt_lo = sb("wdt_lo", [P, R])
        wdt_hi = sb("wdt_hi", [DH, R])
        wdtp = sb("wdtp", [H + 1, D])
        tanh_bias = sb("tanh_bias", [P, 1])
        ln_bias = sb("ln_bias", [P, 1])
        wraw_lo = sb("wraw_lo", [P, FF])
        wraw_hi = sb("wraw_hi", [DH, FF])
        aw1_row = sb("aw1_row", [P, FF])
        wq1_lo = sb("wq1_lo", [P, FF], bf16)
        wq1_hi = sb("wq1_hi", [DH, FF], bf16)
        w2raw = sb("w2raw", [P, FC, D])
        aw2_row = sb("aw2_row", [P, D])
        raw2_row = sb("raw2_row", [P, D])
        wq2 = sb("wq2", [P, FC, D], bf16)
        aa1_row = sb("aa1_row", [P, D])
        aa2_row = sb("aa2_row", [P, FF])
        a1 = sb("a1", [P, 1])
        a2 = sb("a2", [P, 1])
        inv_a1 = sb("inv_a1", [P, 1])
        inv_a2 = sb("inv_a2", [P, 1])
        aw1_col = sb("aw1_col", [P, FC])
        up_scale = sb("up_scale", [P, FC])
        up_bias = sb("up_bias", [P, FC])
        down_scale = sb("down_scale", [P, D])
        down_bias = sb("down_bias", [P, D])

        idx = sb("idx", [P, JB], i32)
        vid_b = sb("vid_b", [NV, S], i32)
        onehot = sb("onehot", [NV, S])
        feat = sb("feat", [P, JB, IN])
        select = sb("select", [P, JB, SEL])
        special = sb("special", [P, JB])
        run = sb("run", [P, JB, CW])
        fprod = sb("fprod", [P, JB, 2, NF])
        gprod = sb("gprod", [P, JB, 2, NG])
        same = sb("same", [P, JB, 2, 2])
        floor = sb("floor", [P, JB])
        rfloor = sb("rfloor", [P, JB])
        stat1 = sb("stat1", [P, JB, 6])
        mv1 = sb("mv1", [P, JB, 2])
        rstd1 = sb("rstd1", [P, JB])
        xhat = sb("xhat", [P, JB, IN])
        xhatT = sb("xhatT", [IN, S])
        hidT = sb("hidT", [H + 1, S])
        h0 = sb("h0", [P, JB, D])
        stat2 = sb("stat2", [P, JB, 6])
        mv2 = sb("mv2", [P, JB, 2])
        rstd2 = sb("rstd2", [P, JB])
        xn = sb("xn", [P, JB, D])
        xT_lo = sb("xT_lo", [P, S])
        xT_hi = sb("xT_hi", [DH, S])
        dtT = sb("dtT", [H + 1, S])
        bc = sb("bc", [P, JB, 2 * N])
        b_cur = sb("b_cur", [P, JB, N])
        soft = sb("soft", [P, JB, D])
        delta = sb("delta", [P, JB, D])
        junk = sb("junk", [P, JB, D])
        sumsq = sb("sumsq", [P, JB])
        rrms = sb("rrms", [P, JB])
        lnd = sb("lnd", [P, JB, 2 * P])
        root = sb("root", [P, JB, D])
        s = sb("s", [P, JB, D])
        skip0 = sb("skip0", [P, JB, D])
        lndT_lo = sb("lndT_lo", [P, S])
        lndT_hi = sb("lndT_hi", [P, S])
        w = sb("w", [P, WR, JB, TG, P])
        abar = sb("abar", [P, AR, S])
        e = sb("e", [P, ER, S])
        c_cur = sb("c_cur", [P, JB, N])
        cb = sb("cb", [P, JB, N])
        kappa = sb("kappa", [P, JB])
        acc = sb("acc", [P, JB, D])
        h1 = sb("h1", [P, JB, D])
        stat3 = sb("stat3", [P, JB, 6])
        mv3 = sb("mv3", [P, JB, 2])
        rstd3 = sb("rstd3", [P, JB])
        xq_raw = sb("xq_raw", [P, JB, D])
        xq = sb("xq", [P, JB, D], bf16)
        xqT = sb("xqT", [P, 2, S], bf16)
        up = sb("up", [P, FC, S])
        hq = sb("hq", [P, FC, S], bf16)
        h1b = sb("h1b", [P, JB, D])
        y = sb("y", [P, JB, D])

        v_ps = ctx.enter_context(nc.psum_tensor("v_ps", [P, 2, 512], f32))
        e_ps = ctx.enter_context(nc.psum_tensor("e_ps", [P, JB, 512], f32))
        side = ctx.enter_context(nc.psum_tensor("side", [P, 2, 512], f32))
        side_bf = side[:, :, :].bitcast(bf16)

        k_load = sem("k_load")
        k_step = sem("k_step")
        passed = sem("passed")
        k_ffn_step = sem("k_ffn_step")
        k_pool = sem("k_pool")
        k_made = sem("k_made")
        k_bias = sem("k_bias")
        k_ffn = sem("k_ffn")
        k_ffn_load = sem("k_ffn_load")
        v_ready = sem("v_ready")
        a_ready = sem("a_ready")
        scan_done = sem("scan_done")
        eT_ready = sem("eT_ready")
        w_ready = sem("w_ready")
        acc_step = sem("acc_step")
        vid_in = sem("vid_in")
        idx_done = sem("idx_done")
        gathered = sem("gathered")
        onehot_done = sem("onehot_done")
        var_mm = sem("var_mm")
        var_done = sem("var_done")
        mask_done = sem("mask_done")
        run_done = sem("run_done")
        cum_mm = sem("cum_mm")
        cum_copied = sem("cum_copied")
        cum_done = sem("cum_done")
        stat1_done = sem("stat1_done")
        rstd1_done = sem("rstd1_done")
        xhat_done = sem("xhat_done")
        xhatT_mm = sem("xhatT_mm")
        xhatT_done = sem("xhatT_done")
        hid_mm = sem("hid_mm")
        hid_done = sem("hid_done")
        h0_mm = sem("h0_mm")
        h0_done = sem("h0_done")
        stat2_done = sem("stat2_done")
        rstd2_done = sem("rstd2_done")
        xn_done = sem("xn_done")
        xT_mm = sem("xT_mm")
        xT_done = sem("xT_done")
        dtbc_mm = sem("dtbc_mm")
        dtbc_done = sem("dtbc_done")
        pre_mm = sem("pre_mm")
        soft_log = sem("soft_log")
        soft_done = sem("soft_done")
        sumsq_done = sem("sumsq_done")
        clamp_done = sem("clamp_done")
        bcur_done = sem("bcur_done")
        rrms_done = sem("rrms_done")
        delta_done = sem("delta_done")
        lnd_done = sem("lnd_done")
        root_done = sem("root_done")
        lndT_mm = sem("lndT_mm")
        lndT_done = sem("lndT_done")
        xin_mm = sem("xin_mm")
        s_done = sem("s_done")
        skip_done = sem("skip_done")
        c_done = sem("c_done")
        stat3_done = sem("stat3_done")
        rstd3_done = sem("rstd3_done")
        xq_done = sem("xq_done")
        xqT_mm = sem("xqT_mm")
        xqT_done = sem("xqT_done")
        up_mm = sem("up_mm")
        up_done = sem("up_done")
        hq1_done = sem("hq1_done")
        hq2_done = sem("hq2_done")
        hq_done = sem("hq_done")
        down_mm = sem("down_mm")
        scaled = sem("scaled")
        h1b_done = sem("h1b_done")
        y_done = sem("y_done")
        stored = sem("stored")

        def after(eng, semaphore, value):
            if not isinstance(value, int) or value > 0:
                eng.wait_ge(semaphore, value)

        def let_pass(eng):
            eng.sem_inc(passed, 1)

        def passes(eng, body):
            body(-1, main=False, front=True, back=False)
            body(0, main=True, front=True, back=False)
            body(1, main=True, front=True, back=True)
            with eng.Fori(2, BATCH - 1) as b:
                body(b, main=True, front=True, back=True)
            body(BATCH - 1, main=True, front=False, back=True)
            body(BATCH, main=False, front=False, back=True)

        CONST_LOADS = 24
        FFN_LOADS = 7
        POOL_CONSTS = 23
        UP_SLOT = {6: [(0, 1)], 8: [(1, 1)], 10: [(2, 0)], 11: [(3, 1)], 12: [(4, 0)], 17: [(5, 0)]}
        UP_NEEDS = [0, 1, 2, 2, 3, 5]

        block = ctx.enter_context(nc.Block())

        @block.sync
        def _(sp):
            def const(dst, src):
                sp.dma_start(dst, src).then_inc(k_load, 16)

            const(tok_sb[:, :], tok_ids)
            const(var_table[:, 0:NF], fam_onehot)
            const(var_table[:, NF:VW], var_cols)
            const(vint[:, :], var_int)
            const(gamma_sb[:, :], ln_gamma)
            const(beta_sb[:, :], ln_beta)
            const(w1_sb[:, :], W1)
            const(b1_sb[:, :], b1)
            const(w2_sb[0:H, :], W2)
            const(w2_sb[H:H + 1, :], b2)
            const(scale_sb[:, :], tok_scale[0:1, :].broadcast_to([H + 1, 1]))
            const(abias_lo[:, :], A_log_lo)
            const(abias_hi[:, :], A_log_hi)
            const(d_row[:, :], D_param[0:1, :].broadcast_to([P, D]))
            const(rms_row[:, :], rms_scale[0:1, :].broadcast_to([P, D]))
            const(wbc_lo[:, :], W_bc[0:P, :])
            const(wbc_hi[:, :], W_bc[P:D, :])
            const(wdt_lo[:, :], W_dt[0:P, :])
            const(wdt_hi[:, :], W_dt[P:D, :])
            sp.wait_ge(k_pool, POOL_CONSTS)
            const(wdtp[0:R, :], W_dtp)
            const(wdtp[H:H + 1, :], b_dt)
            const(aw1_col[:, :], alpha_w1_col)
            const(up_bias[:, :], ffn_b1)
            const(down_bias[:, :], ffn_b2[0:1, :].broadcast_to([P, D]))

            def ffn_const(dst, src):
                sp.dma_start(dst, src).then_inc(k_ffn_load, 16)

            def body(b, main, front, back):
                if front:
                    after(sp, onehot_done, b + 1)
                    sp.dma_start(vid_b[:, :], var_ids[bass.ds(b + 1, 1), :].broadcast_to([NV, S])).then_inc(vid_in, 16)
                if isinstance(b, int) and b == -1:
                    ffn_const(wraw_lo[:, :], ffn_w1T[0:P, :])
                    ffn_const(wraw_hi[:, :], ffn_w1T[P:D, :])
                    ffn_const(aw1_row[:, :], alpha_w1_row[0:1, :].broadcast_to([P, FF]))
                    ffn_const(aa1_row[:, :], alpha_a1[0:1, :].broadcast_to([P, D]))
                    ffn_const(aa2_row[:, :], alpha_a2[0:1, :].broadcast_to([P, FF]))
                    ffn_const(aw2_row[:, :], alpha_w2[0:1, :].broadcast_to([P, D]))
                    ffn_const(w2raw[:, :, :], ffn_w2T.rearrange("(c p) d -> p c d", p=P))
                if back:
                    sp.wait_ge(y_done, b)
                    sp.dma_start(out[bass.ds(b - 1, 1), :, :].rearrange("o (j p) d -> p (o j) d", p=P),
                                 y[:, :, :]).then_inc(stored, 16)

            passes(sp, body)
            sp.wait_ge(stored, 16 * BATCH)

        @block.gpsimd
        def _(pool):
            made = [0]

            def const(ins):
                made[0] += 1
                ins.then_inc(k_pool, 1)

            def select_where(tile, width, base, fill, op=ALU.not_equal, step=-1, mult=1):
                pool.wait_ge(k_pool, made[0])
                const(pool.affine_select(out=tile, in_=tile, compare_op=op, fill=fill, base=base,
                                         pattern=[[step, width]], channel_multiplier=mult))

            for tile, value in ((ident, 0.0), (ident_bf, 0.0), (bidiag, 0.0), (before, 0.0), (ones, 1.0),
                                (shift, 0.0), (edge, 0.0), (avg, 0.0), (avg_edge, 0.0), (wdtp, 0.0), (dtT, 0.0)):
                const(pool.memset(tile[:, :], value))
            select_where(ident[:, :], P, 0, 1.0)
            select_where(ident_bf[:, :], P, 0, 1.0)
            select_where(bidiag[:, :], P + 1, 0, 1.0)
            select_where(bidiag[:, :], P + 1, 1, 1.0)
            select_where(before[:, :], P, 0, 1.0, op=ALU.is_ge)
            select_where(shift[:, :], P, 1, 1.0)
            select_where(edge[:, :], P, -(P - 1), 1.0)
            select_where(avg[:, :], P, 0, 0.25)
            select_where(avg[:, :], P, 1, 0.25)
            select_where(avg_edge[:, :], P, -(P - 1), 0.25)
            const(pool.iota(row_id[:, :], pattern=[[0, 1]], base=0, channel_multiplier=1,
                            allow_small_or_imprecise_dtypes=True))
            const(pool.iota(col_id[:, :], pattern=[[1, NG]], base=0, channel_multiplier=0,
                            allow_small_or_imprecise_dtypes=True))
            assert made[0] == POOL_CONSTS
            pool.iota(feat[:, :, VW + NT], pattern=[[P, JB]], base=0, channel_multiplier=1,
                      allow_small_or_imprecise_dtypes=True).then_inc(k_pool, 1)
            pool.memset(minus_half[:, :], -0.5).then_inc(k_pool, 1)
            pool.wait_ge(k_pool, POOL_CONSTS + 2)
            pool.memset(hidT[H:H + 1, :], 1.0).then_inc(k_pool, 1)
            pool.wait_ge(k_pool, POOL_CONSTS + 3)
            pool.memset(dtT[H:H + 1, :], 1.0).then_inc(k_pool, 1)
            pool.wait_ge(k_pool, POOL_CONSTS + 4)
            pool.memset(tanh_bias[:, :], -MID / HALF).then_inc(k_pool, 1)
            pool.memset(ln_bias[:, :], MID).then_inc(k_pool, 1)
            pool.wait_ge(k_pool, POOL_CONSTS + 6)
            pool.wait_ge(k_load, 16 * CONST_LOADS)

            def power(dst, var, eps, scale, done, value):
                let_pass(pool)
                pool.tensor_scalar(dst, var, scale, eps, ALU.mult, ALU.add).then_inc(done, 1)
                pool.wait_ge(done, value - 1)
                pool.tensor_tensor(dst, dst, minus_half[:, :], ALU.pow).then_inc(done, 1)

            def build_w(b, g):
                slot = g % WR
                if g == 0:
                    pool.wait_ge(dtbc_done, b + 1)
                    after(pool, w_ready, GROUPS * b)
                    let_pass(pool)
                    pool.tensor_copy(b_cur[:, :, :], bc[:, :, 0:N]).then_inc(bcur_done, 1)
                    pool.wait_ge(bcur_done, b + 1)
                    pool.wait_ge(s_done, b + 1)
                after(pool, v_ready, TILES * b + TG * (g - WR + 1))
                pool.tensor_tensor(
                    w[:, slot, :, 0:2, :],
                    s[:, :, 0:P].unsqueeze(2).broadcast_to([P, JB, 2, P]),
                    b_cur[:, :, 2 * g:2 * g + 2].unsqueeze(3).broadcast_to([P, JB, 2, P]), ALU.mult)
                pool.tensor_tensor(
                    w[:, slot, :, 2, :].rearrange("p j (a d) -> p j a d", a=2),
                    s[:, :, P:D].unsqueeze(2).broadcast_to([P, JB, 2, DH]),
                    b_cur[:, :, 2 * g:2 * g + 2].unsqueeze(3).broadcast_to([P, JB, 2, DH]),
                    ALU.mult).then_inc(w_ready, 1)

            def body(b, main, front, back):
                for k in range(TILES):
                    if main and k % TG == 1 and k < TILES - 2 * TG:
                        build_w(b, k // TG + 2)
                    if front and k == 0:
                        after(pool, mask_done, 3 * (b + 1))
                        pool.tensor_copy(idx[:, :], tok_sb[:, bass.ds((b + 1) * JB, JB)]).then_inc(idx_done, 1)
                        after(pool, xhat_done, b + 1)
                        pool.wait_ge(idx_done, b + 2)
                        let_pass(pool)
                        for j in range(JB):
                            pool.indirect_dma_start(
                                out=feat[:, j, 0:NT], out_offset=None, in_=tok_table,
                                in_offset=bass.IndirectOffsetOnAxis(ap=idx[:, j:j + 1], axis=0)).then_inc(gathered, 16)
                    if back and k == 2:
                        pool.wait_ge(k_ffn, 1)
                        pool.wait_ge(stat3_done, 2 * b)
                        power(rstd3[:, :], mv3[:, :, 1], LN_EPS, 1.0, rstd3_done, 3 * b - 1)
                        pool.wait_ge(rstd3_done, 3 * b - 1)
                        let_pass(pool)
                        pool.tensor_scalar(rstd3[:, :], rstd3[:, :], inv_a1[:, 0:1], None, ALU.mult).then_inc(rstd3_done, 1)
                        after(pool, y_done, b - 1)
                        pool.tensor_tensor(h1b[:, :, :], h1[:, :, :],
                                           down_bias[:, :].unsqueeze(1).broadcast_to([P, JB, D]), ALU.add).then_inc(h1b_done, 1)
                    if front and k == 5:
                        pool.wait_ge(stat1_done, 2 * (b + 2))
                        power(rstd1[:, :], mv1[:, :, 1], LN_EPS, 1.0, rstd1_done, 2 * (b + 2))
                    if front and k == 11:
                        pool.wait_ge(stat2_done, 2 * (b + 2))
                        power(rstd2[:, :], mv2[:, :, 1], LN_EPS, 1.0, rstd2_done, 2 * (b + 2))
                    if back and k in (13, 19):
                        half = 0 if k == 13 else 1
                        part = up[:, half * (FC // 2):(half + 1) * (FC // 2), :]
                        pool.wait_ge(hq1_done, 2 * b - 1 + half)
                        let_pass(pool)
                        pool.tensor_scalar(part, part, QP, QN, ALU.min, ALU.max).then_inc(hq2_done, 1)
                    if front and k == 14:
                        after(pool, acc_step, ACC * b + JB)
                        pool.wait_ge(xn_done, b + 2)
                        pool.tensor_tensor(skip0[:, :, :], xn[:, :, :],
                                           d_row[:, :].unsqueeze(1).broadcast_to([P, JB, D]), ALU.mult).then_inc(skip_done, 1)
                        pool.wait_ge(skip_done, 2 * (b + 2) - 1)
                        pool.tensor_tensor(skip0[:, :, :], skip0[:, :, :], h0[:, :, :], ALU.add).then_inc(skip_done, 1)
                    if front and k == 17:
                        pool.wait_ge(sumsq_done, b + 2)
                        power(rrms[:, :], sumsq[:, :], RMS_EPS, 1.0 / D, rrms_done, 2 * (b + 2))
                    if front and k in (21, 22):
                        build_w(b + 1, k - 21)
                    if back and k == 23:
                        pool.wait_ge(scaled, b)
                        after(pool, stored, 16 * (b - 1))
                        pool.tensor_tensor(y[:, :, :], xq_raw[:, :, :], h1b[:, :, :], ALU.add).then_inc(y_done, 1)

            passes(pool, body)

        @block.scalar
        def _(act):
            act.wait_ge(k_pool, POOL_CONSTS + 6)
            act.wait_ge(k_load, 16 * CONST_LOADS)
            act.wait_ge(k_made, 1)

            def make_abar(b, k):
                g, r = divmod(k, TG)
                tile = TILES * b + k
                after(act, scan_done, tile - AR + 1)
                if k == 0:
                    act.wait_ge(lndT_done, b + 1)
                src, bias = (lndT_lo, abias_lo[:, 2 * g + r:2 * g + r + 1]) if r < 2 else (lndT_hi, abias_hi[:, g:g + 1])
                nc.scalar.activation(abar[:, k % AR, :], src[:, :], ACT.Tanh, bias=bias, scale=-0.5).then_inc(a_ready, 1)

            def body(b, main, front, back):
                for k in range(TILES):
                    ahead = k + AR - 1
                    if main and ahead < TILES:
                        make_abar(b, ahead)
                    if front and ahead >= TILES:
                        make_abar(b + 1, ahead - TILES)
                    if front and k == 1:
                        act.wait_ge(var_mm, b + 2)
                        after(act, xhat_done, b + 1)
                        ps = side[:, 0, 0:JB * (VW + SEL)].rearrange("p (j f) -> p j f", j=JB)
                        nc.scalar.copy(feat[:, :, NT:NT + VW], ps[:, :, 0:VW])
                        nc.scalar.copy(select[:, :, :], ps[:, :, VW:VW + SEL]).then_inc(var_done, 1)
                    if front and k == 4:
                        act.wait_ge(cum_mm, b + 2)
                        ps = side[:, 1, 0:JB * CW].rearrange("p (j f) -> p j f", j=JB)
                        prev = side[:, 1, JB * CW:JB * (CW + 2)].rearrange("p (j f) -> p j f", j=JB)
                        nc.scalar.mul(feat[:, :, NT + VW + 1:NT + VW + 3], ps[:, :, 0:2], INV_LEN)
                        nc.scalar.copy(feat[:, :, IN - 2:IN], prev).then_inc(cum_copied, 1)
                    if back and k == 5:
                        act.wait_ge(xqT_mm, b)
                        nc.scalar.copy(xqT[:, 0, :], side_bf[:, 0, 0:S])
                        nc.scalar.copy(xqT[0:DH, 1, :], side_bf[0:DH, 0, S:2 * S]).then_inc(xqT_done, 1)
                    if back and k in UP_SLOT:
                        for c, bank in UP_SLOT[k]:
                            act.wait_ge(up_mm, FC * (b - 1) + c + 1)
                            if c == 0:
                                after(act, hq_done, 2 * (b - 1))
                            nc.scalar.activation(up[:, c, :], side[:, bank, :], ACT.Gelu, bias=up_bias[:, c:c + 1],
                                                 scale=up_scale[:, c:c + 1]).then_inc(up_done, 1)
                    if front and k == 7:
                        act.wait_ge(xhatT_mm, b + 2)
                        nc.scalar.copy(xhatT[:, :], side[0:IN, 0, :]).then_inc(xhatT_done, 1)
                    if front and k == 8:
                        act.wait_ge(hid_mm, b + 2)
                        nc.scalar.activation(hidT[0:H, :], side[0:H, 0, :], ACT.Gelu, bias=bias1[:, 0:1]).then_inc(hid_done, 1)
                    if front and k == 9:
                        act.wait_ge(h0_mm, b + 2)
                        after(act, skip_done, 2 * (b + 1))
                        nc.scalar.copy(h0[:, :, :].rearrange("p (a j) d -> p a (j d)", a=2),
                                       side[:, :, 0:2 * D]).then_inc(h0_done, 1)
                    if front and k == 13:
                        act.wait_ge(xT_mm, b + 2)
                        nc.scalar.copy(xT_lo[:, :], side[:, 0, :])
                        nc.scalar.copy(xT_hi[:, :], side[0:DH, 1, :]).then_inc(xT_done, 1)
                    if front and k == 14:
                        act.wait_ge(dtbc_mm, b + 2)
                        nc.scalar.copy(dtT[0:R, :], side[0:R, 0, :])
                        after(act, bcur_done, b + 1)
                        after(act, c_done, 3 * (b + 1))
                        nc.scalar.copy(bc[:, :, :], side[:, 1, 0:JB * 2 * N].rearrange("p (j n) -> p j n", j=JB)).then_inc(dtbc_done, 1)
                    if front and k == 15:
                        act.wait_ge(pre_mm, b + 2)
                        flat = soft[:, :, :].rearrange("p (a j) d -> p a (j d)", a=2)
                        after(act, delta_done, b + 1)
                        let_pass(act)
                        nc.scalar.preload_act_table_set("natural_log_exp_and_others")
                        nc.scalar.activation(flat, side[:, :, 0:2 * D], ACT.Abs).then_inc(soft_log, 1)
                        act.wait_ge(soft_log, 3 * (b + 1) + 1)
                        nc.scalar.activation(flat, flat, ACT.Exp, scale=-1.0).then_inc(soft_log, 1)
                        act.wait_ge(soft_log, 3 * (b + 1) + 2)
                        nc.scalar.activation(flat, flat, ACT.Ln, bias=1.0).then_inc(soft_log, 1)
                        nc.scalar.preload_act_table_set("gelu_and_others")
                    if front and k == 17:
                        act.wait_ge(soft_done, b + 2)
                        for j in range(JB):
                            last = nc.scalar.activation(junk[:, j, :], soft[:, j, :], ACT.Square, accum_out=sumsq[:, j:j + 1])
                        last.then_inc(sumsq_done, 1)
                    if front and k == 18:
                        act.wait_ge(delta_done, b + 2)
                        nc.scalar.activation(delta[:, :, :], delta[:, :, :], ACT.Tanh, bias=tanh_bias[:, 0:1],
                                             scale=1.0 / HALF).then_inc(clamp_done, 1)
                        nc.scalar.preload_act_table_set("natural_log_exp_and_others")
                        act.wait_ge(clamp_done, b + 2)
                        nc.scalar.activation(lnd[:, :, 0:D], delta[:, :, :], ACT.Ln, bias=ln_bias[:, 0:1], scale=HALF)
                        nc.scalar.activation(lnd[:, :, D:2 * P], delta[:, :, P:D], ACT.Ln, bias=ln_bias[:, 0:1],
                                             scale=HALF).then_inc(lnd_done, 1)
                        act.wait_ge(lnd_done, b + 2)
                        after(act, s_done, b + 1)
                        nc.scalar.activation(root[:, :, :], lnd[:, :, 0:D], ACT.Exp, scale=0.5).then_inc(root_done, 1)
                        nc.scalar.preload_act_table_set("gelu_and_others")
                    if front and k == 20:
                        act.wait_ge(lndT_mm, b + 2)
                        after(act, a_ready, TILES * (b + 1))
                        nc.scalar.copy(lndT_lo[:, :], side[:, 0, :])
                        nc.scalar.copy(lndT_hi[:, :], side[:, 1, :]).then_inc(lndT_done, 1)

            passes(act, body)

        @block.vector
        def _(dve):
            dve.wait_ge(k_pool, POOL_CONSTS + 6)
            dve.wait_ge(k_load, 16 * CONST_LOADS)
            nc.vector.tensor_copy(vintf[:, :], vint[:, :]).then_inc(k_step, 1)
            dve.wait_ge(k_step, 1)
            nc.vector.tensor_scalar(vgrp[:, :], vintf[:, 1:2], 0.0, None, ALU.is_gt).then_inc(k_step, 1)
            dve.wait_ge(k_step, 2)
            nc.vector.tensor_scalar(var_table[:, VW:VW + NF], col_id[:, 0:NF], vintf[:, 0:1], None, ALU.is_equal)
            nc.vector.tensor_scalar(var_table[:, VW + NF:VW + SEL], col_id[:, :], vintf[:, 1:2], vgrp[:, 0:1],
                                    ALU.is_equal, ALU.mult)
            nc.vector.tensor_scalar(feat[:, :, VW + NT], feat[:, :, VW + NT], INV_LEN, None, ALU.mult)
            nc.vector.tensor_scalar(w1g[:, :], w1_sb[:, :], gamma_sb[:, 0:1], None, ALU.mult)
            nc.vector.tensor_scalar(w2_sb[:, :], w2_sb[:, :], scale_sb[:, 0:1], None, ALU.mult)
            nc.vector.tensor_scalar(abias_lo[:, :], abias_lo[:, :], -0.5, 0.5 * math.log(2.0), ALU.mult, ALU.add)
            nc.vector.tensor_scalar(abias_hi[:, :], abias_hi[:, :], -0.5, 0.5 * math.log(2.0), ALU.mult, ALU.add)
            dve.wait_ge(k_bias, 1)
            nc.vector.tensor_tensor(bias1[:, :], side[0:H, 0, 0:1], b1_sb[:, :], ALU.add).then_inc(k_made, 1)
            dve.wait_ge(k_made, 1)

            def scan(b, k):
                tile = TILES * b + k
                dve.wait_ge(v_ready, tile + 1)
                dve.wait_ge(a_ready, tile + 1)
                after(dve, eT_ready, tile - ER + 1)
                nc.vector.tensor_tensor_scan(e[:, k % ER, :], v_ps[:, k % 2, :], abar[:, k % AR, :], 0.0,
                                             ALU.add, ALU.mult).then_inc(scan_done, 1)

            def accumulate(b, g, nn):
                n = 2 * g + nn
                dve.wait_ge(eT_ready, TILES * b + TG * (g + 1))
                if n == N - 1:
                    after(dve, h1b_done, b)
                for j in range(JB):
                    step = ACC * b + JB * (1 + n) + j
                    dve.wait_ge(acc_step, step - JB + 1)
                    dst = acc if n < N - 1 else h1
                    nc.vector.scalar_tensor_tensor(dst[:, j, :], e_ps[:, j, nn * D:(nn + 1) * D], c_cur[:, j, n:n + 1],
                                                   acc[:, j, :], ALU.mult, ALU.add).then_inc(acc_step, 1)

            def statistics(src, stat, mv, done, value):
                for j in range(JB):
                    last = nc.vector.bn_stats(stat[:, j, :], src[:, j, :])
                last.then_inc(done, 1)
                dve.wait_ge(done, value - 1)
                let_pass(dve)
                for j in range(JB):
                    last = nc.vector.bn_aggr(mv[:, j, :], stat[:, j, :])
                last.then_inc(done, 1)

            def prepare_ffn():
                count = [0]

                def link(ins):
                    count[0] += 1
                    ins.then_inc(k_ffn_step, 1)
                    dve.wait_ge(k_ffn_step, count[0])

                dve.wait_ge(k_ffn_load, 16 * FFN_LOADS)
                link(nc.vector.reciprocal(aw1_row[:, :], aw1_row[:, :]))
                link(nc.vector.reciprocal(raw2_row[:, :], aw2_row[:, :]))
                for raw, inv, quant in (
                        (wraw_lo[:, :], aw1_row[:, :], wq1_lo[:, :]),
                        (wraw_hi[:, :], aw1_row[0:DH, :], wq1_hi[:, :]),
                        (w2raw[:, :, :], raw2_row[:, :].unsqueeze(1).broadcast_to([P, FC, D]), wq2[:, :, :])):
                    link(nc.vector.tensor_tensor(raw, raw, inv, ALU.mult))
                    link(nc.vector.tensor_scalar(raw, raw, QP, QN, ALU.min, ALU.max))
                    link(nc.vector.tensor_scalar(quant, raw, MAGIC, MAGIC, ALU.add, ALU.subtract))
                link(nc.vector.reduce_sum(a1[:, :], aa1_row[:, :], axis=AXX))
                link(nc.vector.reduce_sum(a2[:, :], aa2_row[:, :], axis=AXX))
                link(nc.vector.tensor_scalar(a1[:, :], a1[:, :], 1.0 / D, None, ALU.mult))
                link(nc.vector.tensor_scalar(a2[:, :], a2[:, :], 1.0 / FF, None, ALU.mult))
                link(nc.vector.reciprocal(inv_a1[:, :], a1[:, :]))
                link(nc.vector.reciprocal(inv_a2[:, :], a2[:, :]))
                link(nc.vector.tensor_scalar(up_scale[:, :], aw1_col[:, :], a1[:, 0:1], None, ALU.mult))
                nc.vector.tensor_scalar(down_scale[:, :], aw2_row[:, :], a2[:, 0:1], None, ALU.mult).then_inc(k_ffn, 1)

            def body(b, main, front, back):
                for k in range(TILES):
                    if main:
                        scan(b, k)
                        if k >= TG and k % TG == 0:
                            accumulate(b, k // TG - 1, 0)
                            accumulate(b, k // TG - 1, 1)
                    if back and k == 0:
                        accumulate(b - 1, GROUPS - 1, 0)
                        accumulate(b - 1, GROUPS - 1, 1)
                    if isinstance(b, int) and b == 0 and k == 3:
                        prepare_ffn()
                    if main and k == 2:
                        dve.wait_ge(dtbc_done, b + 1)
                        after(dve, acc_step, ACC * b)
                        nc.vector.tensor_copy(c_cur[:, :, :], bc[:, :, N:2 * N]).then_inc(c_done, 1)
                        nc.vector.tensor_tensor(cb[:, :, :], bc[:, :, 0:N], bc[:, :, N:2 * N], ALU.mult).then_inc(c_done, 1)
                        dve.wait_ge(c_done, 3 * b + 2)
                        nc.vector.reduce_sum(kappa[:, :], cb[:, :, :], axis=AXX).then_inc(c_done, 1)
                        dve.wait_ge(c_done, 3 * b + 3)
                        dve.wait_ge(skip_done, 2 * (b + 1))
                        for j in range(JB):
                            nc.vector.scalar_tensor_tensor(acc[:, j, :], s[:, j, :], kappa[:, j:j + 1], skip0[:, j, :],
                                                           ALU.mult, ALU.add).then_inc(acc_step, 1)
                    if front and k == 0:
                        dve.wait_ge(vid_in, 16 * (b + 2))
                        nc.vector.tensor_scalar(onehot[:, :], vid_b[:, :], row_id[:, 0:1], None, ALU.is_equal).then_inc(onehot_done, 1)
                    if back and k == 1:
                        dve.wait_ge(acc_step, ACC * b)
                        statistics(h1, stat3, mv3, stat3_done, 2 * b)
                    if front and k == 2:
                        dve.wait_ge(idx_done, b + 2)
                        nc.vector.tensor_scalar(special[:, :], idx[:, :], 3.0, None, ALU.is_ge).then_inc(mask_done, 1)
                        dve.wait_ge(mask_done, 3 * (b + 1) + 1)
                        dve.wait_ge(gathered, 16 * JB * (b + 2))
                        after(dve, cum_mm, b + 1)
                        nc.vector.scalar_tensor_tensor(run[:, :, 0], feat[:, :, 0], 0.0, special[:, :],
                                                       ALU.is_gt, ALU.mult).then_inc(mask_done, 1)
                        dve.wait_ge(mask_done, 3 * (b + 1) + 2)
                        nc.vector.tensor_tensor(run[:, :, 1], feat[:, :, 1], run[:, :, 0], ALU.mult).then_inc(mask_done, 1)
                        dve.wait_ge(mask_done, 3 * (b + 1) + 3)
                        dve.wait_ge(var_done, b + 2)
                        nc.vector.tensor_tensor(
                            run[:, :, 2:2 + 2 * NF].rearrange("p j (a f) -> p j a f", a=2),
                            feat[:, :, NT:NT + NF].unsqueeze(2).broadcast_to([P, JB, 2, NF]),
                            run[:, :, 0:2].unsqueeze(3).broadcast_to([P, JB, 2, NF]), ALU.mult)
                        nc.vector.tensor_tensor(
                            run[:, :, 2 + 2 * NF:CW].rearrange("p j (a f) -> p j a f", a=2),
                            select[:, :, NF:SEL].unsqueeze(2).broadcast_to([P, JB, 2, NG]),
                            run[:, :, 0:2].unsqueeze(3).broadcast_to([P, JB, 2, NG]), ALU.mult).then_inc(run_done, 1)
                    if back and k == 3:
                        dve.wait_ge(rstd3_done, 3 * b)
                        after(dve, y_done, b - 1)
                        for j in range(JB):
                            last = nc.vector.tensor_scalar(xq_raw[:, j, :], h1[:, j, :], mv3[:, j, 0:1], rstd3[:, j:j + 1],
                                                           ALU.subtract, ALU.mult)
                        last.then_inc(xq_done, 1)
                        dve.wait_ge(xq_done, 3 * b - 2)
                        nc.vector.tensor_scalar(xq_raw[:, :, :], xq_raw[:, :, :], QP, QN, ALU.min, ALU.max).then_inc(xq_done, 1)
                        dve.wait_ge(xq_done, 3 * b - 1)
                        nc.vector.tensor_scalar(xq[:, :, :], xq_raw[:, :, :], MAGIC, MAGIC, ALU.add, ALU.subtract).then_inc(xq_done, 1)
                    if front and k == 4:
                        base = 3 * (b + 1)
                        dve.wait_ge(cum_mm, b + 2)
                        dve.wait_ge(cum_copied, b + 2)
                        ps = side[:, 1, 0:JB * CW].rearrange("p (j f) -> p j f", j=JB)
                        nc.vector.tensor_scalar(floor[:, :], ps[:, :, 0], 1.0, None, ALU.max)
                        nc.vector.tensor_tensor(
                            fprod[:, :, :, :], ps[:, :, 2:2 + 2 * NF].rearrange("p j (a f) -> p j a f", a=2),
                            select[:, :, 0:NF].unsqueeze(2).broadcast_to([P, JB, 2, NF]), ALU.mult)
                        nc.vector.tensor_tensor(
                            gprod[:, :, :, :], ps[:, :, 2 + 2 * NF:CW].rearrange("p j (a f) -> p j a f", a=2),
                            select[:, :, NF:SEL].unsqueeze(2).broadcast_to([P, JB, 2, NG]), ALU.mult).then_inc(cum_done, 1)
                        dve.wait_ge(cum_done, base + 1)
                        nc.vector.reciprocal(rfloor[:, :], floor[:, :])
                        nc.vector.reduce_sum(same[:, :, 0, :], fprod[:, :, :, :], axis=AXX)
                        nc.vector.reduce_sum(same[:, :, 1, :], gprod[:, :, :, :], axis=AXX).then_inc(cum_done, 1)
                        dve.wait_ge(cum_done, base + 2)
                        dyn = feat[:, :, NT + VW + 3:NT + VW + 9].rearrange("p j (a f) -> p j a f", a=2)
                        nc.vector.tensor_scalar(dyn[:, :, :, 0:2], same[:, :, :, :], INV_LEN, None, ALU.mult)
                        nc.vector.tensor_tensor(dyn[:, :, :, 2], same[:, :, :, 0],
                                                rfloor[:, :].unsqueeze(2).broadcast_to([P, JB, 2]), ALU.mult).then_inc(cum_done, 1)
                    if front and k == 5:
                        dve.wait_ge(cum_done, 3 * (b + 2))
                        statistics(feat, stat1, mv1, stat1_done, 2 * (b + 2))
                    if front and k == 6:
                        dve.wait_ge(rstd1_done, 2 * (b + 2))
                        for j in range(JB):
                            last = nc.vector.tensor_scalar(xhat[:, j, :], feat[:, j, :], mv1[:, j, 0:1], rstd1[:, j:j + 1],
                                                           ALU.subtract, ALU.mult)
                        last.then_inc(xhat_done, 1)
                    if front and k == 11:
                        dve.wait_ge(h0_done, b + 2)
                        statistics(h0, stat2, mv2, stat2_done, 2 * (b + 2))
                    if front and k == 12:
                        dve.wait_ge(rstd2_done, 2 * (b + 2))
                        for j in range(JB):
                            last = nc.vector.tensor_scalar(xn[:, j, :], h0[:, j, :], mv2[:, j, 0:1], rstd2[:, j:j + 1],
                                                           ALU.subtract, ALU.mult)
                        last.then_inc(xn_done, 1)
                    if back and k in (12, 18):
                        half = 0 if k == 12 else 1
                        part = up[:, half * (FC // 2):(half + 1) * (FC // 2), :]
                        dve.wait_ge(up_done, FC * (b - 1) + (half + 1) * (FC // 2))
                        nc.vector.tensor_scalar(part, part, 10.0, inv_a2[:, 0:1], ALU.min, ALU.mult).then_inc(hq1_done, 1)
                    if back and k in (14, 21):
                        half = 0 if k == 14 else 1
                        part = slice(half * (FC // 2), (half + 1) * (FC // 2))
                        dve.wait_ge(hq2_done, 2 * b - 1 + half)
                        nc.vector.tensor_scalar(hq[:, part, :], up[:, part, :], MAGIC, MAGIC, ALU.add,
                                                ALU.subtract).then_inc(hq_done, 1)
                    if front and k == 16:
                        dve.wait_ge(soft_log, 3 * (b + 2))
                        flat = soft[:, :, :].rearrange("p (a j) d -> p a (j d)", a=2)
                        nc.vector.scalar_tensor_tensor(flat, side[:, :, 0:2 * D], 0.0, flat, ALU.max, ALU.add).then_inc(soft_done, 1)
                    if front and k == 18:
                        dve.wait_ge(rrms_done, 2 * (b + 2))
                        for j in range(JB):
                            last = nc.vector.scalar_tensor_tensor(delta[:, j, :], soft[:, j, :], rrms[:, j:j + 1], rms_row[:, :],
                                                                  ALU.mult, ALU.mult)
                        last.then_inc(delta_done, 1)
                    if front and k == 20:
                        dve.wait_ge(xin_mm, b + 2)
                        dve.wait_ge(root_done, b + 2)
                        after(dve, w_ready, GROUPS * (b + 1))
                        nc.vector.tensor_tensor(s[:, :, :].rearrange("p (a j) d -> p a (j d)", a=2), side[:, :, 0:2 * D],
                                                root[:, :, :].rearrange("p (a j) d -> p a (j d)", a=2),
                                                ALU.mult).then_inc(s_done, 1)
                    if back and k == 23:
                        dve.wait_ge(down_mm, b)
                        nc.vector.tensor_tensor(xq_raw[:, :, :].rearrange("p (a j) d -> p a j d", a=2),
                                                side[:, :, 0:2 * D].rearrange("p a (j d) -> p a j d", j=2),
                                                down_scale[:, :].unsqueeze(1).unsqueeze(1).broadcast_to([P, 2, 2, D]),
                                                ALU.mult).then_inc(scaled, 1)

            passes(dve, body)

        @block.tensor
        def _(pe):
            pe.wait_ge(k_pool, POOL_CONSTS + 6)
            pe.wait_ge(k_load, 16 * CONST_LOADS)
            nc.tensor.matmul(side[0:H, 0, 0:1], w1_sb[:, :], beta_sb[:, :], start=True, stop=True).then_inc(k_bias, 1)
            pe.wait_ge(k_made, 1)

            def weigh(b, k):
                g, r = divmod(k, TG)
                tile = TILES * b + k
                if r == 0:
                    pe.wait_ge(w_ready, GROUPS * b + g + 1)
                after(pe, scan_done, tile - 1)
                for j in range(JB):
                    cols = P + 1 if j < JB - 1 else P
                    last = nc.tensor.matmul(v_ps[:, k % 2, j * P:j * P + cols], w[:, g % WR, j, r, :], bidiag[:, 0:cols],
                                            start=(j == 0), stop=(j == JB - 1), skip_group_check=True)
                last.then_inc(v_ready, 1)

            def turn(b, k):
                g, r = divmod(k, TG)
                pe.wait_ge(scan_done, TILES * b + k + 1)
                if r == 0:
                    after(pe, acc_step, ACC * b + JB * (1 + 2 * g) if g else ACC * b)
                for j in range(JB):
                    dst = (e_ps[:, j, r * D:r * D + P] if r < 2
                           else e_ps[:, j, 0:2 * D].rearrange("p (a d) -> p a d", a=2)[:, :, P:D])
                    last = nc.tensor.transpose(dst, e[:, k % ER, j * P:(j + 1) * P], ident[:, :])
                last.then_inc(eT_ready, 1)

            def body(b, main, front, back):
                for k in range(TILES):
                    if main and k + 1 < TILES:
                        weigh(b, k + 1)
                    if front and k + 1 == TILES:
                        weigh(b + 1, 0)
                    if front and k == 1:
                        pe.wait_ge(onehot_done, b + 2)
                        after(pe, s_done, b + 1)
                        after(pe, scaled, b - 1)
                        for j in range(JB):
                            last = nc.tensor.matmul(side[:, 0, j * (VW + SEL):(j + 1) * (VW + SEL)],
                                                    onehot[:, j * P:(j + 1) * P], var_table[:, :], start=True, stop=True)
                        last.then_inc(var_mm, 1)
                    if front and k == 3:
                        pe.wait_ge(run_done, b + 2)
                        sums = side[:, 1, 0:JB * CW]
                        for back_by in range(JB):
                            last = nc.tensor.matmul(
                                side[:, 1, back_by * CW:JB * CW],
                                before[:, :] if back_by == 0 else ones[:, :],
                                run[:, 0:JB - back_by, :], start=(back_by == 0), stop=(back_by == JB - 1),
                                skip_group_check=True)
                        prev = side[:, 1, JB * CW:JB * (CW + 2)]
                        nc.tensor.matmul(prev, shift[:, :], feat[:, :, 1:3], start=False, stop=False, skip_group_check=True)
                        nc.tensor.matmul(side[:, 1, JB * CW + 2:JB * (CW + 2)], edge[:, :], feat[:, 0:JB - 1, 1:3],
                                         start=False, stop=True, skip_group_check=True).then_inc(cum_mm, 1)
                    if back and k == 5:
                        pe.wait_ge(xq_done, 3 * b)
                        pe.wait_ge(k_ffn, 1)
                        if front:
                            pe.wait_ge(var_done, b + 2)
                        else:
                            after(pe, scaled, b - 1)
                            pe.wait_ge(s_done, BATCH)
                        for j in range(JB):
                            nc.tensor.transpose(side_bf[:, 0, j * P:(j + 1) * P], xq[:, j, 0:P], ident_bf[:, :])
                        for j in range(JB):
                            last = nc.tensor.transpose(side_bf[0:DH, 0, S + j * P:S + (j + 1) * P], xq[:, j, P:D], ident_bf[:, :])
                        last.then_inc(xqT_mm, 1)
                    if front and k == 7:
                        pe.wait_ge(xhat_done, b + 2)
                        if back:
                            pe.wait_ge(xqT_done, b)
                        let_pass(pe)
                        for j in range(JB):
                            last = nc.tensor.transpose(side[0:IN, 0, j * P:(j + 1) * P], xhat[:, j, :], ident[:, :])
                        last.then_inc(xhatT_mm, 1)
                    if front and k == 8:
                        pe.wait_ge(xhatT_done, b + 2)
                        let_pass(pe)
                        nc.tensor.matmul(side[0:H, 0, :], w1g[:, :], xhatT[:, :], start=True, stop=True).then_inc(hid_mm, 1)
                    if front and k == 9:
                        pe.wait_ge(hid_done, b + 2)
                        if back:
                            pe.wait_ge(up_done, FC * (b - 1) + 2)
                        for j in range(JB):
                            last = nc.tensor.matmul(side[:, j // 2, (j % 2) * D:(j % 2 + 1) * D], hidT[:, j * P:(j + 1) * P],
                                                    w2_sb[:, :], start=True, stop=True)
                        last.then_inc(h0_mm, 1)
                    if front and k == 13:
                        pe.wait_ge(xn_done, b + 2)
                        if back:
                            pe.wait_ge(up_done, FC * (b - 1) + 5)
                        for j in range(JB):
                            nc.tensor.transpose(side[:, 0, j * P:(j + 1) * P], xn[:, j, 0:P], ident[:, :])
                        for j in range(JB):
                            last = nc.tensor.transpose(side[0:DH, 1, j * P:(j + 1) * P], xn[:, j, P:D], ident[:, :])
                        last.then_inc(xT_mm, 1)
                    if front and k == 14:
                        pe.wait_ge(xT_done, b + 2)
                        nc.tensor.matmul(side[0:R, 0, :], wdt_lo[:, :], xT_lo[:, :], start=True, stop=False)
                        nc.tensor.matmul(side[0:R, 0, :], wdt_hi[:, :], xT_hi[:, :], start=False, stop=True)
                        for j in range(JB):
                            dst = side[:, 1, j * 2 * N:(j + 1) * 2 * N]
                            nc.tensor.matmul(dst, xT_lo[:, j * P:(j + 1) * P], wbc_lo[:, :], start=True, stop=False)
                            last = nc.tensor.matmul(dst, xT_hi[:, j * P:(j + 1) * P], wbc_hi[:, :], start=False, stop=True)
                        last.then_inc(dtbc_mm, 1)
                    if front and k == 15:
                        pe.wait_ge(dtbc_done, b + 2)
                        for j in range(JB):
                            last = nc.tensor.matmul(side[:, j // 2, (j % 2) * D:(j % 2 + 1) * D], dtT[:, j * P:(j + 1) * P],
                                                    wdtp[:, :], start=True, stop=True)
                        last.then_inc(pre_mm, 1)
                    if front and k == 19:
                        pe.wait_ge(lnd_done, b + 2)
                        if back:
                            pe.wait_ge(up_done, FC * b)
                        for j in range(JB):
                            nc.tensor.transpose(side[:, 0, j * P:(j + 1) * P], lnd[:, j, 0:P], ident[:, :])
                        for j in range(JB):
                            last = nc.tensor.transpose(side[:, 1, j * P:(j + 1) * P], lnd[:, j, P:2 * P], ident[:, :])
                        last.then_inc(lndT_mm, 1)
                    if front and k == 20:
                        pe.wait_ge(lndT_done, b + 2)
                        for a in range(2):
                            nc.tensor.matmul(side[:, a, 0:2 * D], avg[:, :], xn[:, 2 * a:2 * a + 2, :], start=True, stop=False,
                                             skip_group_check=True)
                        nc.tensor.matmul(side[:, 0, D:2 * D], avg_edge[:, :], xn[:, 0, :], start=False, stop=True,
                                         skip_group_check=True)
                        nc.tensor.matmul(side[:, 1, 0:2 * D], avg_edge[:, :], xn[:, 1:3, :], start=False, stop=True,
                                         skip_group_check=True).then_inc(xin_mm, 1)
                    if back and k in UP_SLOT:
                        for c, bank in UP_SLOT[k]:
                            up_matmul(b, c, bank, front)
                    if back and k == 22:
                        pe.wait_ge(hq_done, 2 * b)
                        if front:
                            pe.wait_ge(s_done, b + 2)
                        for j in range(JB):
                            for c in range(FC):
                                last = nc.tensor.matmul(side[:, j // 2, (j % 2) * D:(j % 2 + 1) * D], hq[:, c, j * P:(j + 1) * P],
                                                        wq2[:, c, :], start=(c == 0), stop=(c == FC - 1))
                        last.then_inc(down_mm, 1)
                    if main:
                        turn(b, k)

            def up_matmul(b, c, bank, front):
                if c == 0:
                    pe.wait_ge(xqT_done, b)
                    if front:
                        pe.wait_ge(cum_done, 3 * (b + 2))
                elif c == 2 and front:
                    pe.wait_ge(h0_done, b + 2)
                elif c == 5 and front:
                    pe.wait_ge(soft_done, b + 2)
                after(pe, up_done, FC * (b - 1) + UP_NEEDS[c])
                nc.tensor.matmul(side[:, bank, :], wq1_lo[:, c * P:(c + 1) * P], xqT[:, 0, :], start=True, stop=False)
                nc.tensor.matmul(side[:, bank, :], wq1_hi[:, c * P:(c + 1) * P], xqT[0:DH, 1, :], start=False,
                                 stop=True).then_inc(up_mm, 1)

            passes(pe, body)


_OUT_SHAPE = (16, 512, 192)


def kernel(**inputs):
    import numpy as _np
    import concourse.bacc as _bacc
    from concourse import mybir as _mybir
    from concourse.bass_utils import run_bass_kernel_spmd as _run

    t = {k[len("L0_tok_"):]: _np.asarray(v) for k, v in inputs.items() if k.startswith("L0_tok_")}
    a = {k[len("L0_attn_"):]: _np.asarray(v) for k, v in inputs.items() if k.startswith("L0_attn_")}
    f = {k[len("L0_ffn_"):]: _np.asarray(v) for k, v in inputs.items() if k.startswith("L0_ffn_")}
    row = lambda v: v.reshape(1, -1)
    col = lambda v: v.reshape(-1, 1)
    lanes = lambda v: v.reshape(-1, 128).T
    A_log = a["A_log"]
    order = [0, 2, 1] + list(range(3, t["W1"].shape[0]))
    arrays = dict(
        tok_ids=lanes(_np.asarray(inputs["x"])), var_ids=_np.asarray(inputs["itok_BS_0_511"]),
        tok_table=_np.stack([t["token_" + n] for n in ("has_int", "log_norm", "signed_norm", "is_zero", "is_one", "is_pow2")], 1),
        fam_onehot=t["var_family_onehot"],
        var_cols=_np.stack([t["var_" + n] for n in ("outer_norm", "inner_norm", "has_outer", "has_inner")], 1),
        var_int=_np.stack([t["var_family_id"], t["var_group_id"]], 1),
        ln_gamma=col(t["ln_gamma"][order]), ln_beta=col(t["ln_beta"][order]), W1=t["W1"][order], b1=col(t["b1"]), W2=t["W2"], b2=row(t["b2"]),
        tok_scale=t["scale"].reshape(1, 1),
        A_log_lo=A_log[:128], A_log_hi=_np.concatenate([A_log[128:, 0::2], A_log[128:, 1::2]], 0),
        D_param=row(a["D_param"]), W_bc=a["W_bc"], W_dt=a["W_dt"], W_dtp=a["W_dtp"], b_dt=row(a["b_dt"]),
        rms_scale=row(a["rms_scale"]),
        ffn_w1T=f["w1"].T, ffn_b1=lanes(f["b1"]), alpha_w1_col=lanes(f["alpha_w1"]), alpha_w1_row=row(f["alpha_w1"]),
        alpha_a1=row(f["alpha_a1"]), ffn_w2T=f["w2"].T, ffn_b2=row(f["b2"]), alpha_w2=row(f["alpha_w2"]),
        alpha_a2=row(f["alpha_a2"]))
    nc = _bacc.Bacc("TRN2", target_bir_lowering=False, num_devices=1)
    fed, args = {}, {}
    for name, v in arrays.items():
        fed[f"in_{name}"] = _np.ascontiguousarray(v)
        args[name] = nc.dram_tensor(f"in_{name}", v.shape, _mybir.dt.from_np(v.dtype), kind="ExternalInput").ap()
    args["out"] = nc.dram_tensor("out_h", _OUT_SHAPE, _mybir.dt.float32, kind="ExternalOutput").ap()
    lm_tower_kernel(nc, **args)
    r = _run(nc, [fed], core_ids=[0])
    return r.results[0]["out_h"]
```

```python
import concourse.bass as bass
from concourse import mybir
from contextlib import ExitStack
import math


def lm_tower_kernel(
    nc: bass.Bass,
    tok_ids: bass.AP,
    var_ids: bass.AP,
    tok_table: bass.AP,
    fam_onehot: bass.AP,
    var_cols: bass.AP,
    var_int: bass.AP,
    ln_gamma: bass.AP,
    ln_beta: bass.AP,
    W1: bass.AP,
    b1: bass.AP,
    W2: bass.AP,
    b2: bass.AP,
    tok_scale: bass.AP,
    A_log_lo: bass.AP,
    A_log_hi: bass.AP,
    D_param: bass.AP,
    W_bc: bass.AP,
    W_dt: bass.AP,
    W_dtp: bass.AP,
    b_dt: bass.AP,
    rms_scale: bass.AP,
    ffn_w1T: bass.AP,
    ffn_b1: bass.AP,
    alpha_w1_col: bass.AP,
    alpha_w1_row: bass.AP,
    alpha_a1: bass.AP,
    ffn_w2T: bass.AP,
    ffn_b2: bass.AP,
    alpha_w2: bass.AP,
    alpha_a2: bass.AP,
    out: bass.AP,
):
    f32, bf16, i32 = mybir.dt.float32, mybir.dt.bfloat16, mybir.dt.int32
    ALU = mybir.AluOpType
    ACT = mybir.ActivationFunctionType
    AXX = mybir.AxisListType.X

    P = 128
    BATCH, S = var_ids.shape
    JB = S // P
    NV, NF = fam_onehot.shape
    NG = 32
    IN, H = W1.shape
    D = W2.shape[1]
    DH = D - P
    N = A_log_lo.shape[1]
    R = W_dt.shape[1]
    XR = -(-(2 * N + R) // 32) * 32
    FF = ffn_w1T.shape[1]
    FC = FF // P
    NT = 6
    VW = NF + 4
    SEL = NF + NG
    CW = 2 + 2 * NF + 2 * NG
    GROUPS = N // 2
    TG = 3
    TILES = GROUPS * TG
    WR, AR, ER = 4, 6, 6
    BY_ACT = (2,5)
    ACC = JB * (1 + N - 2 * len(BY_ACT))
    LO, HI = 0.0001, 10.0
    MID, HALF = (HI + LO) / 2.0, (HI - LO) / 2.0
    MAGIC = 12582912.0
    QN, QP = -8.0, 7.0
    INV_LEN = 1.0 / float(S - 1)
    LN_EPS, RMS_EPS = 1e-5, 1e-6

    ctx = ExitStack()
    with ctx:
        def sb(name, shape, dt=f32):
            return ctx.enter_context(nc.sbuf_tensor(name, shape, dt))

        def sem(name):
            return ctx.enter_context(nc.semaphore(name))

        ident = sb("ident", [P, P])
        ident_bf = sb("ident_bf", [P, P], bf16)
        bidiag = sb("bidiag", [P, P + 1])
        before = sb("before", [P, P])
        ones = sb("ones", [P, P])
        shift = sb("shift", [P, P])
        edge = sb("edge", [P, P])
        avg = sb("avg", [P, P])
        avg_edge = sb("avg_edge", [P, P])
        row_id = sb("row_id", [P, 1])
        col_id = sb("col_id", [P, NG])
        cap = sb("cap", [P, 1])
        minus_half = sb("minus_half", [P, JB])
        tok_sb = sb("tok_sb", [P, BATCH * JB], i32)
        var_table = sb("var_table", [NV, VW + SEL])
        vint = sb("vint", [NV, 2], i32)
        vintf = sb("vintf", [NV, 2])
        vgrp = sb("vgrp", [NV, 1])
        gamma_sb = sb("gamma_sb", [IN, 1])
        beta_sb = sb("beta_sb", [IN, 1])
        w1_sb = sb("w1_sb", [IN, H])
        w1g = sb("w1g", [IN, H])
        b1_sb = sb("b1_sb", [H, 1])
        bias1 = sb("bias1", [H, 1])
        w2_sb = sb("w2_sb", [H + 1, D])
        scale_sb = sb("scale_sb", [H + 1, 1])
        abias_lo = sb("abias_lo", [P, N])
        abias_hi = sb("abias_hi", [P, N // 2])
        d_row = sb("d_row", [P, D])
        rms_row = sb("rms_row", [P, D])
        wx_lo = sb("wx_lo", [P, XR])
        wx_hi = sb("wx_hi", [DH, XR])
        wdtp = sb("wdtp", [XR + 1, D])
        wraw_lo = sb("wraw_lo", [P, FF])
        wraw_hi = sb("wraw_hi", [DH, FF])
        aw1_row = sb("aw1_row", [P, FF])
        wq1_lo = sb("wq1_lo", [P, FF], bf16)
        wq1_hi = sb("wq1_hi", [DH, FF], bf16)
        w2raw = sb("w2raw", [P, FC, D])
        aw2_row = sb("aw2_row", [P, D])
        raw2_row = sb("raw2_row", [P, D])
        wq2 = sb("wq2", [P, FC, D], bf16)
        aa1_row = sb("aa1_row", [P, D])
        aa2_row = sb("aa2_row", [P, FF])
        a1 = sb("a1", [P, 1])
        a2 = sb("a2", [P, 1])
        inv_a1 = sb("inv_a1", [P, 1])
        inv_a2 = sb("inv_a2", [P, 1])
        aw1_col = sb("aw1_col", [P, FC])
        up_scale = sb("up_scale", [P, FC])
        up_bias = sb("up_bias", [P, FC])
        down_scale = sb("down_scale", [P, D])
        down_bias = sb("down_bias", [P, D])

        idx = sb("idx", [P, JB], i32)
        vid_b = sb("vid_b", [NV, S], i32)
        onehot = sb("onehot", [NV, S])
        feat = sb("feat", [P, JB, IN])
        select = sb("select", [P, JB, SEL])
        special = sb("special", [P, JB])
        run = sb("run", [P, JB, CW])
        fprod = sb("fprod", [P, JB, 2, NF])
        gprod = sb("gprod", [P, JB, 2, NG])
        same = sb("same", [P, JB, 2, 2])
        floor = sb("floor", [P, JB])
        rfloor = sb("rfloor", [P, JB])
        stat1 = sb("stat1", [P, JB, 6])
        mv1 = sb("mv1", [P, JB, 2])
        rstd1 = sb("rstd1", [P, JB])
        xhat = sb("xhat", [P, JB, IN])
        xhatT = sb("xhatT", [IN, S])
        hidT = sb("hidT", [H + 1, S])
        h0 = sb("h0", [P, JB, D])
        stat2 = sb("stat2", [P, JB, 6])
        mv2 = sb("mv2", [P, JB, 2])
        rstd2 = sb("rstd2", [P, JB])
        xn = sb("xn", [P, JB, D])
        xT_lo = sb("xT_lo", [P, S])
        xT_hi = sb("xT_hi", [DH, S])
        bcdtT = sb("bcdtT", [XR + 1, S])
        bc = sb("bc", [P, JB, 2 * N])
        b_cur = sb("b_cur", [P, JB, N])
        z = sb("z", [P, JB, D])
        soft = sb("soft", [P, JB, D])
        delta = sb("delta", [P, JB, D])
        junk = sb("junk", [P, JB, D])
        sumsq = sb("sumsq", [P, JB])
        rrms = sb("rrms", [P, JB])
        lnd = sb("lnd", [P, JB, 2 * P])
        root = sb("root", [P, JB, D])
        xin = sb("xin", [P, JB, D])
        s = sb("s", [P, JB, D])
        skip0 = sb("skip0", [P, JB, D])
        lndT_lo = sb("lndT_lo", [P, S])
        lndT_hi = sb("lndT_hi", [P, S])
        w = sb("w", [P, WR, JB, TG, P])
        abar = sb("abar", [P, AR, S])
        e = sb("e", [P, ER, S])
        c_next = sb("c_next", [P, JB, N])
        c_cur = sb("c_cur", [P, JB, N])
        cb = sb("cb", [P, JB, N])
        kappa = sb("kappa", [P, JB])
        acc = sb("acc", [P, JB, D])
        prod = sb("prod", [P, 2, JB, D])
        h1 = sb("h1", [P, JB, D])
        stat3 = sb("stat3", [P, JB, 6])
        mv3 = sb("mv3", [P, JB, 2])
        rstd3 = sb("rstd3", [P, JB])
        xq_raw = sb("xq_raw", [P, JB, D])
        xq = sb("xq", [P, JB, D], bf16)
        xqT = sb("xqT", [P, 2, S], bf16)
        up = sb("up", [P, FC, S])
        hq = sb("hq", [P, FC, S], bf16)
        h1b = sb("h1b", [P, JB, D])
        y = sb("y", [P, JB, D])

        v_ps = ctx.enter_context(nc.psum_tensor("v_ps", [P, 2, 512], f32))
        e_ps = ctx.enter_context(nc.psum_tensor("e_ps", [P, JB, 512], f32))
        side = ctx.enter_context(nc.psum_tensor("side", [P, 2, 512], f32))
        side_bf = side[:, :, :].bitcast(bf16)

        k_tok = sem("k_tok")
        k_load = sem("k_load")
        k_step = sem("k_step")
        passed = sem("passed")
        k_ffn_step = sem("k_ffn_step")
        k_pool = sem("k_pool")
        k_made = sem("k_made")
        k_bias = sem("k_bias")
        k_ffn = sem("k_ffn")
        k_ffn_load = sem("k_ffn_load")
        v_ready = sem("v_ready")
        a_ready = sem("a_ready")
        scan_done = sem("scan_done")
        eT_ready = sem("eT_ready")
        w_ready = sem("w_ready")
        acc_step = sem("acc_step")
        prod_ready = sem("prod_ready")
        prod_added = sem("prod_added")
        vid_in = sem("vid_in")
        idx_done = sem("idx_done")
        gathered = sem("gathered")
        onehot_done = sem("onehot_done")
        var_mm = sem("var_mm")
        var_done = sem("var_done")
        mask_done = sem("mask_done")
        run_done = sem("run_done")
        cum_mm = sem("cum_mm")
        cum_done = sem("cum_done")
        stat1_done = sem("stat1_done")
        rstd1_done = sem("rstd1_done")
        xhat_done = sem("xhat_done")
        xhatT_mm = sem("xhatT_mm")
        xhatT_done = sem("xhatT_done")
        hid_mm = sem("hid_mm")
        hid_done = sem("hid_done")
        h0_mm = sem("h0_mm")
        h0_done = sem("h0_done")
        stat2_done = sem("stat2_done")
        rstd2_done = sem("rstd2_done")
        xn_done = sem("xn_done")
        xT_mm = sem("xT_mm")
        xT_done = sem("xT_done")
        dtbc_mm = sem("dtbc_mm")
        dtbc_done = sem("dtbc_done")
        bc_done = sem("bc_done")
        pre_mm = sem("pre_mm")
        soft_log = sem("soft_log")
        soft_done = sem("soft_done")
        sumsq_done = sem("sumsq_done")
        clamp_done = sem("clamp_done")
        bcur_done = sem("bcur_done")
        rrms_done = sem("rrms_done")
        delta_done = sem("delta_done")
        lnd_done = sem("lnd_done")
        root_done = sem("root_done")
        lndT_mm = sem("lndT_mm")
        lndT_done = sem("lndT_done")
        xin_mm = sem("xin_mm")
        xin_done = sem("xin_done")
        s_done = sem("s_done")
        skip_done = sem("skip_done")
        c_done = sem("c_done")
        stat3_done = sem("stat3_done")
        rstd3_done = sem("rstd3_done")
        xq_done = sem("xq_done")
        xqT_mm = sem("xqT_mm")
        xqT_done = sem("xqT_done")
        up_mm = sem("up_mm")
        up_done = sem("up_done")
        hq_scaled = sem("hq_scaled")
        hq_done = sem("hq_done")
        down_mm = sem("down_mm")
        scaled = sem("scaled")
        h1b_done = sem("h1b_done")
        y_done = sem("y_done")
        stored = sem("stored")

        def after(eng, semaphore, value):
            if not isinstance(value, int) or value > 0:
                eng.wait_ge(semaphore, value)

        def let_pass(eng):
            eng.sem_inc(passed, 1)

        def passes(eng, body):
            body(-2, head=True, front=False, main=False, back=False)
            body(-1, head=True, front=True, main=False, back=False)
            body(0, head=True, front=True, main=True, back=False)
            body(1, head=True, front=True, main=True, back=True)
            with eng.Fori(2, BATCH - 2) as b:
                body(b, head=True, front=True, main=True, back=True)
            body(BATCH - 2, head=False, front=True, main=True, back=True)
            body(BATCH - 1, head=False, front=False, main=True, back=True)
            body(BATCH, head=False, front=False, main=False, back=True)

        def steps_before(g):
            return JB * (1 + 2 * (g - sum(o < g for o in BY_ACT)))

        CONST_LOADS = 23
        FFN_LOADS = 7
        PREPARE = {(-2, 8): 0, (-2, 16): 1, (-1, 2): 2, (-1, 3): 3, (-1, 4): 4}
        POOL_ZEROS = 3
        POOL_CONSTS = 24
        POOL_ALL = POOL_CONSTS + 4
        UP_SLOT = {8: (0, 1), 9: (1, 1), 12: (2, 1), 14: (3, 1), 15: (4, 1), 16: (5, 1)}

        block = ctx.enter_context(nc.Block())

        @block.sync
        def _(sp):
            def const(dst, src):
                sp.dma_start(dst, src).then_inc(k_load, 16)

            sp.dma_start(tok_sb[:, :], tok_ids).then_inc(k_tok, 16)
            const(var_table[:, 0:NF], fam_onehot)
            const(var_table[:, NF:VW], var_cols)
            const(vint[:, :], var_int)
            const(gamma_sb[:, :], ln_gamma)
            const(beta_sb[:, :], ln_beta)
            const(w1_sb[:, :], W1)
            const(b1_sb[:, :], b1)
            sp.wait_ge(k_pool, POOL_ZEROS)
            const(wx_lo[:, 0:2 * N], W_bc[0:P, :])
            const(wx_hi[:, 0:2 * N], W_bc[P:D, :])
            const(wdtp[2 * N:2 * N + R, :], W_dtp)
            const(wdtp[XR:XR + 1, :], b_dt)

            def ffn_const(dst, src):
                sp.dma_start(dst, src).then_inc(k_ffn_load, 16)

            def body(b, head, front, main, back):
                if head:
                    after(sp, onehot_done, b + 2)
                    sp.dma_start(vid_b[:, :], var_ids[bass.ds(b + 2, 1), :].broadcast_to([NV, S])).then_inc(vid_in, 16)
                if isinstance(b, int) and b == -2:
                    ffn_const(wraw_lo[:, :], ffn_w1T[0:P, :])
                    ffn_const(wraw_hi[:, :], ffn_w1T[P:D, :])
                    ffn_const(aw1_row[:, :], alpha_w1_row[0:1, :].broadcast_to([P, FF]))
                    ffn_const(aa1_row[:, :], alpha_a1[0:1, :].broadcast_to([P, D]))
                    ffn_const(aa2_row[:, :], alpha_a2[0:1, :].broadcast_to([P, FF]))
                    ffn_const(aw2_row[:, :], alpha_w2[0:1, :].broadcast_to([P, D]))
                    ffn_const(w2raw[:, :, :], ffn_w2T.rearrange("(c p) d -> p c d", p=P))
                if not isinstance(b, int) or b >= 2:
                    store(b - 2)

            def store(row):
                sp.wait_ge(y_done, row + 1)
                sp.dma_start(out[bass.ds(row, 1), :, :].rearrange("o (j p) d -> p (o j) d", p=P),
                             y[:, :, :]).then_inc(stored, 16)

            passes(sp, body)
            store(BATCH - 1)
            sp.wait_ge(stored, 16 * BATCH)

        @block.gpsimd
        def _(pool):
            made = [0]

            def const(ins):
                made[0] += 1
                ins.then_inc(k_pool, 1)

            def select_where(tile, width, base, fill, op=ALU.not_equal, step=-1, mult=1):
                pool.wait_ge(k_pool, made[0])
                const(pool.affine_select(out=tile, in_=tile, compare_op=op, fill=fill, base=base,
                                         pattern=[[step, width]], channel_multiplier=mult))

            def gather(b):
                after(pool, mask_done, 3 * (b + 2))
                pool.tensor_copy(idx[:, :], tok_sb[:, bass.ds((b + 2) * JB, JB)]).then_inc(idx_done, 1)
                after(pool, xhat_done, b + 2)
                pool.wait_ge(idx_done, b + 3)
                let_pass(pool)
                for j in range(JB):
                    pool.indirect_dma_start(
                        out=feat[:, j, 0:NT], out_offset=None, in_=tok_table,
                        in_offset=bass.IndirectOffsetOnAxis(ap=idx[:, j:j + 1], axis=0)).then_inc(gathered, 16)

            for tile in (wx_lo, wx_hi, wdtp):
                const(pool.memset(tile[:, :], 0.0))
            assert made[0] == POOL_ZEROS
            pool.wait_ge(k_tok, 16)
            gather(-2)
            for tile, value in ((ident, 0.0), (ident_bf, 0.0), (bidiag, 0.0), (before, 0.0), (ones, 1.0),
                                (shift, 0.0), (edge, 0.0), (avg, 0.0), (avg_edge, 0.0)):
                const(pool.memset(tile[:, :], value))
            select_where(ident[:, :], P, 0, 1.0)
            select_where(ident_bf[:, :], P, 0, 1.0)
            select_where(bidiag[:, :], P + 1, 0, 1.0)
            select_where(bidiag[:, :], P + 1, 1, 1.0)
            select_where(before[:, :], P, 0, 1.0, op=ALU.is_ge)
            select_where(shift[:, :], P, 1, 1.0)
            select_where(edge[:, :], P, -(P - 1), 1.0)
            select_where(avg[:, :], P, 0, 0.25)
            select_where(avg[:, :], P, 1, 0.25)
            select_where(avg_edge[:, :], P, -(P - 1), 0.25)
            const(pool.iota(row_id[:, :], pattern=[[0, 1]], base=0, channel_multiplier=1,
                            allow_small_or_imprecise_dtypes=True))
            const(pool.iota(col_id[:, :], pattern=[[1, NG]], base=0, channel_multiplier=0,
                            allow_small_or_imprecise_dtypes=True))
            assert made[0] == POOL_CONSTS
            pool.iota(feat[:, :, VW + NT], pattern=[[P, JB]], base=0, channel_multiplier=1,
                      allow_small_or_imprecise_dtypes=True).then_inc(k_pool, 1)
            pool.memset(minus_half[:, :], -0.5).then_inc(k_pool, 1)
            pool.wait_ge(k_pool, POOL_CONSTS + 2)
            pool.memset(hidT[H:H + 1, :], 1.0).then_inc(k_pool, 1)
            pool.wait_ge(k_pool, POOL_CONSTS + 3)
            pool.memset(bcdtT[XR:XR + 1, :], 1.0).then_inc(k_pool, 1)
            pool.wait_ge(k_pool, POOL_ALL)
            pool.wait_ge(k_load, 16 * CONST_LOADS)

            def power(dst, var, eps, scale, done, value):
                let_pass(pool)
                pool.tensor_scalar(dst, var, scale, eps, ALU.mult, ALU.add).then_inc(done, 1)
                pool.wait_ge(done, value - 1)
                pool.tensor_tensor(dst, dst, minus_half[:, :], ALU.pow).then_inc(done, 1)

            def build_w(b, g):
                slot = g % WR
                if g == 0:
                    pool.wait_ge(bc_done, b + 1)
                    after(pool, w_ready, GROUPS * b)
                    let_pass(pool)
                    pool.tensor_copy(b_cur[:, :, :], bc[:, :, 0:N]).then_inc(bcur_done, 1)
                    pool.wait_ge(bcur_done, b + 1)
                    pool.wait_ge(s_done, b + 1)
                after(pool, v_ready, TILES * b + TG * (g - WR + 1))
                pool.tensor_tensor(
                    w[:, slot, :, 0:2, :],
                    s[:, :, 0:P].unsqueeze(2).broadcast_to([P, JB, 2, P]),
                    b_cur[:, :, 2 * g:2 * g + 2].unsqueeze(3).broadcast_to([P, JB, 2, P]), ALU.mult)
                pool.tensor_tensor(
                    w[:, slot, :, 2, :].rearrange("p j (a d) -> p j a d", a=2),
                    s[:, :, P:D].unsqueeze(2).broadcast_to([P, JB, 2, DH]),
                    b_cur[:, :, 2 * g:2 * g + 2].unsqueeze(3).broadcast_to([P, JB, 2, DH]),
                    ALU.mult).then_inc(w_ready, 1)

            def add_products(b, g):
                turn_no = BY_ACT.index(g)
                before_it = len(BY_ACT) * b + turn_no
                pool.wait_ge(prod_ready, 2 * before_it + 2)
                pool.wait_ge(acc_step, ACC * b + steps_before(g))
                for nn in range(2):
                    after(pool, prod_added, 2 * before_it + nn)
                    pool.tensor_tensor(acc[:, :, :], acc[:, :, :], prod[:, nn, :, :], ALU.add).then_inc(prod_added, 1)

            def body(b, head, front, main, back):
                for k in range(TILES):
                    if main and k % TG == 2 and k < TILES - 2 * TG:
                        build_w(b, k // TG + 2)
                    if head and k == 0 and not (isinstance(b, int) and b == -2):
                        gather(b)
                    if back and k == 4:
                        pool.wait_ge(k_ffn, 3)
                        pool.wait_ge(stat3_done, 2 * b)
                        power(rstd3[:, :], mv3[:, :, 1], LN_EPS, 1.0, rstd3_done, 3 * b - 1)
                        pool.wait_ge(rstd3_done, 3 * b - 1)
                        let_pass(pool)
                        pool.tensor_scalar(rstd3[:, :], rstd3[:, :], inv_a1[:, 0:1], None, ALU.mult).then_inc(rstd3_done, 1)
                    if back and k == 5:
                        after(pool, y_done, b - 1)
                        pool.tensor_tensor(h1b[:, :, :], h1[:, :, :],
                                           down_bias[:, :].unsqueeze(1).broadcast_to([P, JB, D]), ALU.add).then_inc(h1b_done, 1)
                    if front and k == 8:
                        pool.wait_ge(sumsq_done, b + 2)
                        power(rrms[:, :], sumsq[:, :], RMS_EPS, 1.0 / D, rrms_done, 2 * (b + 2))
                    if head and k == 11:
                        pool.wait_ge(stat1_done, 2 * (b + 3))
                        power(rstd1[:, :], mv1[:, :, 1], LN_EPS, 1.0, rstd1_done, 2 * (b + 3))
                    if front and k == 12:
                        after(pool, acc_step, ACC * b + JB)
                        pool.wait_ge(xn_done, b + 2)
                        pool.tensor_tensor(skip0[:, :, :], xn[:, :, :],
                                           d_row[:, :].unsqueeze(1).broadcast_to([P, JB, D]), ALU.mult).then_inc(skip_done, 1)
                    if front and k == 13:
                        pool.wait_ge(skip_done, 2 * (b + 2) - 1)
                        pool.tensor_tensor(skip0[:, :, :], skip0[:, :, :], h0[:, :, :], ALU.add).then_inc(skip_done, 1)
                    if front and k in (18, 21):
                        build_w(b + 1, (k - 18) // TG)
                    if head and k == 20:
                        pool.wait_ge(stat2_done, 2 * (b + 3))
                        power(rstd2[:, :], mv2[:, :, 1], LN_EPS, 1.0, rstd2_done, 2 * (b + 3))
                    if main and k % TG == 2 and k // TG - 1 in BY_ACT:
                        add_products(b, k // TG - 1)
                    if back and k == 23:
                        pool.wait_ge(scaled, b)
                        after(pool, stored, 16 * (b - 1))
                        after(pool, h1b_done, b)
                        pool.tensor_tensor(y[:, :, :], xq_raw[:, :, :], h1b[:, :, :], ALU.add).then_inc(y_done, 1)

            passes(pool, body)

        @block.scalar
        def _(act):
            def const(dst, src):
                act.dma_start(dst, src).then_inc(k_load, 16)

            const(w2_sb[0:H, :], W2)
            const(w2_sb[H:H + 1, :], b2)
            const(scale_sb[:, :], tok_scale[0:1, :].broadcast_to([H + 1, 1]))
            const(abias_lo[:, :], A_log_lo)
            const(abias_hi[:, :], A_log_hi)
            const(d_row[:, :], D_param[0:1, :].broadcast_to([P, D]))
            const(rms_row[:, :], rms_scale[0:1, :].broadcast_to([P, D]))
            const(aw1_col[:, :], alpha_w1_col)
            const(up_bias[:, :], ffn_b1)
            const(down_bias[:, :], ffn_b2[0:1, :].broadcast_to([P, D]))
            act.wait_ge(k_pool, POOL_ZEROS)
            const(wx_lo[:, 2 * N:2 * N + R], W_dt[0:P, :])
            const(wx_hi[:, 2 * N:2 * N + R], W_dt[P:D, :])
            act.wait_ge(k_pool, POOL_ALL)
            act.wait_ge(k_load, 16 * CONST_LOADS)
            act.wait_ge(k_made, 1)

            def make_abar(b, k):
                g, r = divmod(k, TG)
                tile = TILES * b + k
                after(act, scan_done, tile - AR + 1)
                if k == 0:
                    act.wait_ge(lndT_done, b + 1)
                src, bias = (lndT_lo, abias_lo[:, 2 * g + r:2 * g + r + 1]) if r < 2 else (lndT_hi, abias_hi[:, g:g + 1])
                nc.scalar.activation(abar[:, k % AR, :], src[:, :], ACT.Tanh, bias=bias, scale=-0.5).then_inc(a_ready, 1)

            def products(b, g):
                before_it = len(BY_ACT) * b + BY_ACT.index(g)
                act.wait_ge(c_done, 4 * b + 3)
                after(act, prod_added, 2 * before_it)
                for half in range(2):
                    act.wait_ge(eT_ready, 2 * (GROUPS * b + g) + half + 1)
                    for j in (2 * half, 2 * half + 1):
                        for nn in range(2):
                            n = 2 * g + nn
                            last = nc.scalar.mul(prod[:, nn, j, :], e_ps[:, j, nn * D:(nn + 1) * D], c_cur[:, j, n:n + 1])
                    last.then_inc(prod_ready, 1)

            def clamp(b):
                act.wait_ge(delta_done, b + 2)
                nc.scalar.activation(delta[:, :, :], delta[:, :, :], ACT.Tanh, bias=-MID / HALF,
                                     scale=1.0 / HALF).then_inc(clamp_done, 1)
                nc.scalar.preload_act_table_set("natural_log_exp_and_others")
                act.wait_ge(clamp_done, b + 2)
                after(act, lndT_mm, b + 1)
                nc.scalar.activation(lnd[:, :, 0:D], delta[:, :, :], ACT.Ln, bias=MID, scale=HALF)
                nc.scalar.activation(lnd[:, :, D:2 * P], delta[:, :, P:D], ACT.Ln, bias=MID,
                                     scale=HALF).then_inc(lnd_done, 1)
                act.wait_ge(lnd_done, b + 2)
                after(act, s_done, b + 1)
                nc.scalar.activation(root[:, :, :], lnd[:, :, 0:D], ACT.Exp, scale=0.5).then_inc(root_done, 1)
                nc.scalar.preload_act_table_set("gelu_and_others")

            def copy_lndT(b):
                act.wait_ge(lndT_mm, b + 2)
                after(act, a_ready, TILES * (b + 1))
                nc.scalar.copy(lndT_lo[:, :], side[:, 0, :])
                nc.scalar.copy(lndT_hi[:, :], side[:, 1, :]).then_inc(lndT_done, 1)

            def body(b, head, front, main, back):
                first_front = isinstance(b, int) and b == -1
                for k in range(TILES):
                    ahead = k + 4
                    if main and ahead < TILES:
                        make_abar(b, ahead)
                    if front and ahead >= TILES:
                        make_abar(b + 1, ahead - TILES)
                    if main and k % TG == 1 and k // TG - 1 in BY_ACT:
                        products(b, k // TG - 1)
                    if front and k == 0:
                        act.wait_ge(xT_mm, b + 2)
                        nc.scalar.copy(xT_lo[:, :], side[:, 0, :])
                        nc.scalar.copy(xT_hi[:, :], side[0:DH, 1, :]).then_inc(xT_done, 1)
                    if front and k == 2:
                        act.wait_ge(dtbc_mm, b + 2)
                        nc.scalar.copy(bcdtT[0:XR, :], side[0:XR, 0, :]).then_inc(dtbc_done, 1)
                    if front and k == 3:
                        act.wait_ge(pre_mm, b + 2)
                        flat = soft[:, :, :].rearrange("p (a j) d -> p a (j d)", a=2)
                        after(act, bcur_done, b + 1)
                        after(act, c_done, 4 * b + 2)
                        nc.scalar.copy(bc[:, :, :], side[:, 0, 2 * D:2 * D + JB * 2 * N].rearrange(
                            "p (j n) -> p j n", j=JB)).then_inc(bc_done, 1)
                        after(act, delta_done, b + 1)
                        nc.scalar.copy(z[:, :, :].rearrange("p (a j) d -> p a (j d)", a=2), side[:, :, 0:2 * D])
                        nc.scalar.activation(flat, side[:, :, 0:2 * D], ACT.Abs).then_inc(soft_log, 1)
                        let_pass(act)
                        nc.scalar.preload_act_table_set("natural_log_exp_and_others")
                        act.wait_ge(soft_log, 3 * (b + 1) + 1)
                        nc.scalar.activation(flat, flat, ACT.Exp, scale=-1.0).then_inc(soft_log, 1)
                        act.wait_ge(soft_log, 3 * (b + 1) + 2)
                        nc.scalar.activation(flat, flat, ACT.Ln, bias=1.0).then_inc(soft_log, 1)
                        nc.scalar.preload_act_table_set("gelu_and_others")
                    if head and k == 5:
                        act.wait_ge(var_mm, b + 3)
                        after(act, xhat_done, b + 2)
                        ps = side[:, 0, 0:JB * (VW + SEL)].rearrange("p (j f) -> p j f", j=JB)
                        nc.scalar.copy(feat[:, :, NT:NT + VW], ps[:, :, 0:VW])
                        nc.scalar.copy(select[:, :, :], ps[:, :, VW:VW + SEL]).then_inc(var_done, 1)
                    if front and k == 7:
                        act.wait_ge(soft_done, b + 2)
                        for j in range(JB):
                            last = nc.scalar.activation(junk[:, j, :], soft[:, j, :], ACT.Square, accum_out=sumsq[:, j:j + 1])
                        last.then_inc(sumsq_done, 1)
                    if back and k == 6:
                        act.wait_ge(xqT_mm, b)
                        nc.scalar.copy(xqT[:, 0, :], side_bf[:, 1, 0:S])
                        nc.scalar.copy(xqT[0:DH, 1, :], side_bf[0:DH, 1, S:2 * S]).then_inc(xqT_done, 1)
                    if back and k in UP_SLOT:
                        c, bank = UP_SLOT[k]
                        act.wait_ge(up_mm, FC * (b - 1) + c + 1)
                        if c == 0:
                            after(act, hq_done, 4 * (b - 1))
                        nc.scalar.activation(up[:, c, :], side[:, bank, :], ACT.Gelu, bias=up_bias[:, c:c + 1],
                                             scale=up_scale[:, c:c + 1]).then_inc(up_done, 1)
                    if back and k in (13, 17):
                        half = 0 if k == 13 else 1
                        part = up[:, half * (FC // 2):(half + 1) * (FC // 2), :]
                        act.wait_ge(up_done, FC * (b - 1) + (half + 1) * (FC // 2))
                        nc.scalar.mul(part, part, inv_a2[:, 0:1]).then_inc(hq_scaled, 1)
                    if front and k == 10 and first_front:
                        clamp(b)
                    if front and k == 10:
                        act.wait_ge(xin_mm, b + 2)
                        nc.scalar.copy(xin[:, :, :].rearrange("p (a j) d -> p a (j d)", a=2),
                                       side[:, :, 0:2 * D]).then_inc(xin_done, 1)
                    if front and k == 11:
                        if first_front:
                            copy_lndT(b)
                        else:
                            clamp(b)
                    if head and k == 13:
                        act.wait_ge(xhatT_mm, b + 3)
                        nc.scalar.copy(xhatT[:, :], side[0:IN, 0, :]).then_inc(xhatT_done, 1)
                    if head and k == 15:
                        act.wait_ge(hid_mm, b + 3)
                        nc.scalar.activation(hidT[0:H, :], side[0:H, 0, :], ACT.Gelu, bias=bias1[:, 0:1]).then_inc(hid_done, 1)
                    if head and k == 17:
                        act.wait_ge(h0_mm, b + 3)
                        after(act, skip_done, 2 * (b + 2))
                        nc.scalar.copy(h0[:, :, :].rearrange("p (a j) d -> p a (j d)", a=2),
                                       side[:, :, 0:2 * D]).then_inc(h0_done, 1)
                    if front and k == 19 and not first_front:
                        copy_lndT(b)

            passes(act, body)

        @block.vector
        def _(dve):
            dve.wait_ge(k_pool, POOL_ALL)
            dve.wait_ge(k_load, 16 * CONST_LOADS)
            nc.vector.tensor_copy(vintf[:, :], vint[:, :]).then_inc(k_step, 1)
            dve.wait_ge(k_step, 1)
            nc.vector.tensor_scalar(vgrp[:, :], vintf[:, 1:2], 0.0, None, ALU.is_gt).then_inc(k_step, 1)
            dve.wait_ge(k_step, 2)
            nc.vector.tensor_scalar(var_table[:, VW:VW + NF], col_id[:, 0:NF], vintf[:, 0:1], None, ALU.is_equal)
            nc.vector.tensor_scalar(var_table[:, VW + NF:VW + SEL], col_id[:, :], vintf[:, 1:2], vgrp[:, 0:1],
                                    ALU.is_equal, ALU.mult)
            nc.vector.tensor_scalar(feat[:, :, VW + NT], feat[:, :, VW + NT], INV_LEN, None, ALU.mult)
            nc.vector.tensor_scalar(w1g[:, :], w1_sb[:, :], gamma_sb[:, 0:1], None, ALU.mult)
            nc.vector.tensor_scalar(w2_sb[:, :], w2_sb[:, :], scale_sb[:, 0:1], None, ALU.mult)
            nc.vector.tensor_scalar(abias_lo[:, :], abias_lo[:, :], -0.5, 0.5 * math.log(2.0), ALU.mult, ALU.add)
            nc.vector.tensor_scalar(abias_hi[:, :], abias_hi[:, :], -0.5, 0.5 * math.log(2.0), ALU.mult, ALU.add)
            dve.wait_ge(k_bias, 1)
            nc.vector.tensor_tensor(bias1[:, :], side[0:H, 0, 0:1], b1_sb[:, :], ALU.add).then_inc(k_made, 1)
            dve.wait_ge(k_made, 1)

            def scan(b, k):
                tile = TILES * b + k
                dve.wait_ge(v_ready, tile + 1)
                dve.wait_ge(a_ready, tile + 1)
                after(dve, eT_ready, 2 * (GROUPS * b + k // TG - ER // TG + 1))
                nc.vector.tensor_tensor_scan(e[:, k % ER, :], v_ps[:, k % 2, :], abar[:, k % AR, :], 0.0,
                                             ALU.add, ALU.mult).then_inc(scan_done, 1)

            def accumulate(b, g):
                if g in BY_ACT:
                    return
                for half in range(2):
                    dve.wait_ge(eT_ready, 2 * (GROUPS * b + g) + half + 1)
                    if half == 0:
                        added = sum(o < g for o in BY_ACT)
                        if added:
                            dve.wait_ge(prod_added, 2 * (len(BY_ACT) * b + added))
                        if g == GROUPS - 1:
                            after(dve, h1b_done, b)
                    for nn in range(2):
                        n = 2 * g + nn
                        for j in (2 * half, 2 * half + 1):
                            step = ACC * b + steps_before(g) + JB * half + 2 * nn + j % 2
                            dve.wait_ge(acc_step, step - 1)
                            dst = acc if n < N - 1 else h1
                            nc.vector.scalar_tensor_tensor(dst[:, j, :], e_ps[:, j, nn * D:(nn + 1) * D], c_cur[:, j, n:n + 1],
                                                           acc[:, j, :], ALU.mult, ALU.add).then_inc(acc_step, 1)

            def statistics(src, stat, mv, done, value):
                for j in range(JB):
                    last = nc.vector.bn_stats(stat[:, j, :], src[:, j, :])
                last.then_inc(done, 1)
                dve.wait_ge(done, value - 1)
                let_pass(dve)
                for j in range(JB):
                    last = nc.vector.bn_aggr(mv[:, j, :], stat[:, j, :])
                last.then_inc(done, 1)

            def prepare_ffn(part):
                def link(ins):
                    prepared[0] += 1
                    ins.then_inc(k_ffn_step, 1)
                    dve.wait_ge(k_ffn_step, prepared[0])

                if part == 0:
                    dve.wait_ge(k_ffn_load, 16 * FFN_LOADS)
                    link(nc.vector.reciprocal(raw2_row[:, :], aw2_row[:, :]))
                    link(nc.vector.reduce_sum(a1[:, :], aa1_row[:, :], axis=AXX))
                    link(nc.vector.reduce_sum(a2[:, :], aa2_row[:, :], axis=AXX))
                    link(nc.vector.tensor_scalar(a1[:, :], a1[:, :], 1.0 / D, None, ALU.mult))
                    link(nc.vector.tensor_scalar(a2[:, :], a2[:, :], 1.0 / FF, None, ALU.mult))
                    link(nc.vector.reciprocal(inv_a1[:, :], a1[:, :]))
                    link(nc.vector.reciprocal(inv_a2[:, :], a2[:, :]))
                    link(nc.vector.tensor_scalar(cap[:, :], inv_a2[:, :], 10.0, QP, ALU.mult, ALU.min))
                    link(nc.vector.tensor_scalar(up_scale[:, :], aw1_col[:, :], a1[:, 0:1], None, ALU.mult))
                    link(nc.vector.tensor_scalar(down_scale[:, :], aw2_row[:, :], a2[:, 0:1], None, ALU.mult))
                if part == 1:
                    link(nc.vector.reciprocal(aw1_row[:, :], aw1_row[:, :]))
                if part in (2, 3, 4):
                    raw, inv, quant = (
                        (wraw_lo[:, :], aw1_row[:, :], wq1_lo[:, :]),
                        (wraw_hi[:, :], aw1_row[0:DH, :], wq1_hi[:, :]),
                        (w2raw[:, :, :], raw2_row[:, :].unsqueeze(1).broadcast_to([P, FC, D]), wq2[:, :, :]))[part - 2]
                    link(nc.vector.tensor_tensor(raw, raw, inv, ALU.mult))
                    link(nc.vector.tensor_scalar(raw, raw, QP, QN, ALU.min, ALU.max))
                    nc.vector.tensor_scalar(quant, raw, MAGIC, MAGIC, ALU.add, ALU.subtract).then_inc(k_ffn, 1)

            prepared = [0]

            def body(b, head, front, main, back):
                for k in range(TILES):
                    if main:
                        scan(b, k)
                        if k >= TG and k % TG == 2:
                            accumulate(b, k // TG - 1)
                    if back and k == 2:
                        accumulate(b - 1, GROUPS - 1)
                    if isinstance(b, int) and (b, k) in PREPARE:
                        prepare_ffn(PREPARE[b, k])
                    if main and k == 0:
                        dve.wait_ge(bc_done, b + 1)
                        after(dve, c_done, 4 * b)
                        nc.vector.tensor_copy(c_next[:, :, :], bc[:, :, N:2 * N]).then_inc(c_done, 1)
                        nc.vector.tensor_tensor(cb[:, :, :], bc[:, :, 0:N], bc[:, :, N:2 * N], ALU.mult).then_inc(c_done, 1)
                    if head and k == 0:
                        dve.wait_ge(vid_in, 16 * (b + 3))
                        nc.vector.tensor_scalar(onehot[:, :], vid_b[:, :], row_id[:, 0:1], None, ALU.is_equal).then_inc(onehot_done, 1)
                    if back and k == 3:
                        dve.wait_ge(acc_step, ACC * b)
                        statistics(h1, stat3, mv3, stat3_done, 2 * b)
                    if main and k == 3:
                        after(dve, acc_step, ACC * b)
                        dve.wait_ge(c_done, 4 * b + 2)
                        nc.vector.tensor_copy(c_cur[:, :, :], c_next[:, :, :]).then_inc(c_done, 1)
                        nc.vector.reduce_sum(kappa[:, :], cb[:, :, :], axis=AXX).then_inc(c_done, 1)
                        dve.wait_ge(c_done, 4 * b + 4)
                        dve.wait_ge(skip_done, 2 * (b + 1))
                        for j in range(JB):
                            nc.vector.scalar_tensor_tensor(acc[:, j, :], s[:, j, :], kappa[:, j:j + 1], skip0[:, j, :],
                                                           ALU.mult, ALU.add).then_inc(acc_step, 1)
                    if front and k == 6:
                        dve.wait_ge(soft_log, 3 * (b + 2))
                        nc.vector.scalar_tensor_tensor(soft[:, :, :], z[:, :, :], 0.0, soft[:, :, :], ALU.max,
                                                       ALU.add).then_inc(soft_done, 1)
                    if back and k == 5:
                        dve.wait_ge(rstd3_done, 3 * b)
                        after(dve, y_done, b - 1)
                        for j in range(JB):
                            last = nc.vector.tensor_scalar(xq_raw[:, j, :], h1[:, j, :], mv3[:, j, 0:1], rstd3[:, j:j + 1],
                                                           ALU.subtract, ALU.mult)
                        last.then_inc(xq_done, 1)
                        dve.wait_ge(xq_done, 3 * b - 2)
                        nc.vector.tensor_scalar(xq_raw[:, :, :], xq_raw[:, :, :], QP, QN, ALU.min, ALU.max).then_inc(xq_done, 1)
                        dve.wait_ge(xq_done, 3 * b - 1)
                        nc.vector.tensor_scalar(xq[:, :, :], xq_raw[:, :, :], MAGIC, MAGIC, ALU.add, ALU.subtract).then_inc(xq_done, 1)
                    if head and k == 7:
                        dve.wait_ge(idx_done, b + 3)
                        nc.vector.tensor_scalar(special[:, :], idx[:, :], 3.0, None, ALU.is_ge).then_inc(mask_done, 1)
                        dve.wait_ge(mask_done, 3 * (b + 2) + 1)
                        dve.wait_ge(gathered, 16 * JB * (b + 3))
                        after(dve, cum_mm, b + 2)
                        nc.vector.scalar_tensor_tensor(run[:, :, 0], feat[:, :, 0], 0.0, special[:, :],
                                                       ALU.is_gt, ALU.mult).then_inc(mask_done, 1)
                        dve.wait_ge(mask_done, 3 * (b + 2) + 2)
                        nc.vector.tensor_tensor(run[:, :, 1], feat[:, :, 1], run[:, :, 0], ALU.mult).then_inc(mask_done, 1)
                        dve.wait_ge(mask_done, 3 * (b + 2) + 3)
                        dve.wait_ge(var_done, b + 3)
                        nc.vector.tensor_tensor(
                            run[:, :, 2:2 + 2 * NF].rearrange("p j (a f) -> p j a f", a=2),
                            feat[:, :, NT:NT + NF].unsqueeze(2).broadcast_to([P, JB, 2, NF]),
                            run[:, :, 0:2].unsqueeze(3).broadcast_to([P, JB, 2, NF]), ALU.mult)
                        nc.vector.tensor_tensor(
                            run[:, :, 2 + 2 * NF:CW].rearrange("p j (a f) -> p j a f", a=2),
                            select[:, :, NF:SEL].unsqueeze(2).broadcast_to([P, JB, 2, NG]),
                            run[:, :, 0:2].unsqueeze(3).broadcast_to([P, JB, 2, NG]), ALU.mult).then_inc(run_done, 1)
                    if front and k == 9:
                        dve.wait_ge(rrms_done, 2 * (b + 2))
                        for j in range(JB):
                            last = nc.vector.scalar_tensor_tensor(delta[:, j, :], soft[:, j, :], rrms[:, j:j + 1], rms_row[:, :],
                                                                  ALU.mult, ALU.mult)
                        last.then_inc(delta_done, 1)
                    if head and k == 9:
                        base = 3 * (b + 2)
                        dve.wait_ge(cum_mm, b + 3)
                        ps = side[:, 0, 0:JB * CW].rearrange("p (j f) -> p j f", j=JB)
                        prev = side[:, 0, JB * CW:JB * (CW + 2)].rearrange("p (j f) -> p j f", j=JB)
                        nc.vector.tensor_scalar(feat[:, :, NT + VW + 1:NT + VW + 3], ps[:, :, 0:2], INV_LEN, None, ALU.mult)
                        nc.vector.tensor_copy(feat[:, :, IN - 2:IN], prev)
                        nc.vector.tensor_scalar(floor[:, :], ps[:, :, 0], 1.0, None, ALU.max)
                        nc.vector.tensor_tensor(
                            fprod[:, :, :, :], ps[:, :, 2:2 + 2 * NF].rearrange("p j (a f) -> p j a f", a=2),
                            select[:, :, 0:NF].unsqueeze(2).broadcast_to([P, JB, 2, NF]), ALU.mult)
                        nc.vector.tensor_tensor(
                            gprod[:, :, :, :], ps[:, :, 2 + 2 * NF:CW].rearrange("p j (a f) -> p j a f", a=2),
                            select[:, :, NF:SEL].unsqueeze(2).broadcast_to([P, JB, 2, NG]), ALU.mult).then_inc(cum_done, 1)
                        dve.wait_ge(cum_done, base + 1)
                        nc.vector.reciprocal(rfloor[:, :], floor[:, :])
                        nc.vector.reduce_sum(same[:, :, 0, :], fprod[:, :, :, :], axis=AXX)
                        nc.vector.reduce_sum(same[:, :, 1, :], gprod[:, :, :, :], axis=AXX).then_inc(cum_done, 1)
                        dve.wait_ge(cum_done, base + 2)
                        dyn = feat[:, :, NT + VW + 3:NT + VW + 9].rearrange("p j (a f) -> p j a f", a=2)
                        nc.vector.tensor_scalar(dyn[:, :, :, 0:2], same[:, :, :, :], INV_LEN, None, ALU.mult)
                        nc.vector.tensor_tensor(dyn[:, :, :, 2], same[:, :, :, 0],
                                                rfloor[:, :].unsqueeze(2).broadcast_to([P, JB, 2]), ALU.mult).then_inc(cum_done, 1)
                    if head and k == 11:
                        dve.wait_ge(cum_done, 3 * (b + 3))
                        statistics(feat, stat1, mv1, stat1_done, 2 * (b + 3))
                    if head and k == 12:
                        dve.wait_ge(rstd1_done, 2 * (b + 3))
                        for j in range(JB):
                            last = nc.vector.tensor_scalar(xhat[:, j, :], feat[:, j, :], mv1[:, j, 0:1], rstd1[:, j:j + 1],
                                                           ALU.subtract, ALU.mult)
                        last.then_inc(xhat_done, 1)
                    if back and k in (16, 19):
                        half = 0 if k == 16 else 1
                        part = slice(half * (FC // 2), (half + 1) * (FC // 2))
                        dve.wait_ge(hq_scaled, 2 * b - 1 + half)
                        nc.vector.tensor_scalar(up[:, part, :], up[:, part, :], cap[:, 0:1], QN, ALU.min, ALU.max).then_inc(hq_done, 1)
                        dve.wait_ge(hq_done, 4 * b - 3 + 2 * half)
                        nc.vector.tensor_scalar(hq[:, part, :], up[:, part, :], MAGIC, MAGIC, ALU.add,
                                                ALU.subtract).then_inc(hq_done, 1)
                    if front and k == 17:
                        dve.wait_ge(xin_done, b + 2)
                        dve.wait_ge(root_done, b + 2)
                        after(dve, w_ready, GROUPS * (b + 1))
                        nc.vector.tensor_tensor(s[:, :, :], xin[:, :, :], root[:, :, :], ALU.mult).then_inc(s_done, 1)
                    if head and k == 19:
                        dve.wait_ge(h0_done, b + 3)
                        statistics(h0, stat2, mv2, stat2_done, 2 * (b + 3))
                    if back and k == 23:
                        dve.wait_ge(down_mm, b)
                        nc.vector.tensor_tensor(xq_raw[:, :, :].rearrange("p (a j) d -> p a j d", a=2),
                                                side[:, :, 0:2 * D].rearrange("p a (j d) -> p a j d", j=2),
                                                down_scale[:, :].unsqueeze(1).unsqueeze(1).broadcast_to([P, 2, 2, D]),
                                                ALU.mult).then_inc(scaled, 1)
                    if head and k == 22:
                        dve.wait_ge(rstd2_done, 2 * (b + 3))
                        for j in range(JB):
                            last = nc.vector.tensor_scalar(xn[:, j, :], h0[:, j, :], mv2[:, j, 0:1], rstd2[:, j:j + 1],
                                                           ALU.subtract, ALU.mult)
                        last.then_inc(xn_done, 1)

            passes(dve, body)

        @block.tensor
        def _(pe):
            pe.wait_ge(k_pool, POOL_ALL)
            pe.wait_ge(k_load, 16 * CONST_LOADS)
            nc.tensor.matmul(side[0:H, 0, 0:1], w1_sb[:, :], beta_sb[:, :], start=True, stop=True).then_inc(k_bias, 1)
            pe.wait_ge(k_made, 1)

            def weigh(b, k):
                g, r = divmod(k, TG)
                tile = TILES * b + k
                if r == 0:
                    pe.wait_ge(w_ready, GROUPS * b + g + 1)
                after(pe, scan_done, tile - 1)
                for j in range(JB):
                    cols = P + 1 if j < JB - 1 else P
                    last = nc.tensor.matmul(v_ps[:, k % 2, j * P:j * P + cols], w[:, g % WR, j, r, :], bidiag[:, 0:cols],
                                            start=(j == 0), stop=(j == JB - 1), skip_group_check=True)
                last.then_inc(v_ready, 1)

            def weigh_ahead(b, ahead, front, main):
                if main and ahead < TILES:
                    weigh(b, ahead)
                if front and ahead >= TILES:
                    weigh(b + 1, ahead - TILES)

            def turn(b, g):
                for half in range(2):
                    if g - 1 in BY_ACT:
                        pe.wait_ge(prod_ready, 2 * (len(BY_ACT) * b + BY_ACT.index(g - 1)) + half + 1)
                    else:
                        after(pe, acc_step, ACC * b + (steps_before(g) if g else 0) - JB * (1 - half))
                    if half == 0:
                        pe.wait_ge(scan_done, TILES * b + TG * (g + 1))
                    for r in range(TG):
                        for j in (2 * half, 2 * half + 1):
                            dst = (e_ps[:, j, r * D:r * D + P] if r < 2
                                   else e_ps[:, j, 0:2 * D].rearrange("p (a d) -> p a d", a=2)[:, :, P:D])
                            last = nc.tensor.transpose(dst, e[:, (TG * g + r) % ER, j * P:(j + 1) * P], ident[:, :])
                    last.then_inc(eT_ready, 1)

            def up_matmul(b, c, bank):
                nc.tensor.matmul(side[:, bank, :], wq1_lo[:, c * P:(c + 1) * P], xqT[:, 0, :], start=True, stop=False)
                nc.tensor.matmul(side[:, bank, :], wq1_hi[:, c * P:(c + 1) * P], xqT[0:DH, 1, :], start=False,
                                 stop=True).then_inc(up_mm, 1)

            def turn_lnd(b, head):
                pe.wait_ge(lnd_done, b + 2)
                if isinstance(b, int) and b == -1:
                    pe.wait_ge(xin_done, b + 2)
                elif head:
                    pe.wait_ge(h0_done, b + 3)
                else:
                    pe.wait_ge(up_done, FC * b)
                for j in range(JB):
                    nc.tensor.transpose(side[:, 0, j * P:(j + 1) * P], lnd[:, j, 0:P], ident[:, :])
                for j in range(JB):
                    last = nc.tensor.transpose(side[:, 1, j * P:(j + 1) * P], lnd[:, j, P:2 * P], ident[:, :])
                last.then_inc(lndT_mm, 1)

            def body(b, head, front, main, back):
                first_front = isinstance(b, int) and b == -1
                for k in range(TILES):
                    if main and k and k % TG == 0:
                        turn(b, k // TG - 1)
                    if back and k == 0:
                        turn(b - 1, GROUPS - 1)
                    if k % TG != 1:
                        weigh_ahead(b, k + 2, front, main)
                    if front and k == 0:
                        pe.wait_ge(xn_done, b + 2)
                        after(pe, lndT_done, b + 1)
                        after(pe, scaled, b - 1)
                        for j in range(JB):
                            nc.tensor.transpose(side[:, 0, j * P:(j + 1) * P], xn[:, j, 0:P], ident[:, :])
                        for j in range(JB):
                            last = nc.tensor.transpose(side[0:DH, 1, j * P:(j + 1) * P], xn[:, j, P:D], ident[:, :])
                        last.then_inc(xT_mm, 1)
                    if front and k == 2:
                        pe.wait_ge(xT_done, b + 2)
                        nc.tensor.matmul(side[0:XR, 0, :], wx_lo[:, :], xT_lo[:, :], start=True, stop=False)
                        last = nc.tensor.matmul(side[0:XR, 0, :], wx_hi[:, :], xT_hi[:, :], start=False, stop=True)
                        last.then_inc(dtbc_mm, 1)
                    if front and k == 3:
                        pe.wait_ge(dtbc_done, b + 2)
                        let_pass(pe)
                        for j in range(JB):
                            nc.tensor.transpose(side[:, 0, 2 * D + j * 2 * N:2 * D + (j + 1) * 2 * N],
                                                bcdtT[0:2 * N, j * P:(j + 1) * P], ident[0:2 * N, 0:2 * N])
                        for j in range(JB):
                            last = nc.tensor.matmul(side[:, j // 2, (j % 2) * D:(j % 2 + 1) * D], bcdtT[:, j * P:(j + 1) * P],
                                                    wdtp[:, :], start=True, stop=True)
                        last.then_inc(pre_mm, 1)
                    if head and k == 5:
                        pe.wait_ge(onehot_done, b + 3)
                        if front:
                            pe.wait_ge(soft_log, 3 * (b + 1) + 1)
                        for j in range(JB):
                            last = nc.tensor.matmul(side[:, 0, j * (VW + SEL):(j + 1) * (VW + SEL)],
                                                    onehot[:, j * P:(j + 1) * P], var_table[:, :], start=True, stop=True)
                        last.then_inc(var_mm, 1)
                    if back and k == 6:
                        pe.wait_ge(xq_done, 3 * b)
                        pe.wait_ge(k_ffn, 3)
                        if front:
                            pe.wait_ge(soft_log, 3 * (b + 1) + 1)
                        else:
                            pe.wait_ge(lndT_done, BATCH)
                            pe.wait_ge(scaled, b - 1)
                        for j in range(JB):
                            nc.tensor.transpose(side_bf[:, 1, j * P:(j + 1) * P], xq[:, j, 0:P], ident_bf[:, :])
                        for j in range(JB):
                            last = nc.tensor.transpose(side_bf[0:DH, 1, S + j * P:S + (j + 1) * P], xq[:, j, P:D], ident_bf[:, :])
                        last.then_inc(xqT_mm, 1)
                    if back and k in (8, 9):
                        pe.wait_ge(xqT_done, b)
                        after(pe, up_done, FC * (b - 1) + k - 8)
                        up_matmul(b, *UP_SLOT[k])
                    if head and k == 8:
                        pe.wait_ge(run_done, b + 3)
                        for back_by in range(JB):
                            nc.tensor.matmul(
                                side[:, 0, back_by * CW:JB * CW],
                                before[:, :] if back_by == 0 else ones[:, :],
                                run[:, 0:JB - back_by, :], start=(back_by == 0), stop=(back_by == JB - 1),
                                skip_group_check=True)
                        nc.tensor.matmul(side[:, 0, JB * CW:JB * (CW + 2)], shift[:, :], feat[:, :, 1:3],
                                         start=False, stop=False, skip_group_check=True)
                        nc.tensor.matmul(side[:, 0, JB * CW + 2:JB * (CW + 2)], edge[:, :], feat[:, 0:JB - 1, 1:3],
                                         start=False, stop=True, skip_group_check=True).then_inc(cum_mm, 1)
                    if front and k == 10:
                        if head:
                            pe.wait_ge(cum_done, 3 * (b + 3))
                        if back:
                            pe.wait_ge(up_done, FC * (b - 1) + 2)
                        for a in range(2):
                            nc.tensor.matmul(side[:, a, 0:2 * D], avg[:, :], xn[:, 2 * a:2 * a + 2, :], start=True, stop=False,
                                             skip_group_check=True)
                        nc.tensor.matmul(side[:, 0, D:2 * D], avg_edge[:, :], xn[:, 0, :], start=False, stop=True,
                                         skip_group_check=True)
                        nc.tensor.matmul(side[:, 1, 0:2 * D], avg_edge[:, :], xn[:, 1:3, :], start=False, stop=True,
                                         skip_group_check=True).then_inc(xin_mm, 1)
                    if front and k == 11 and first_front:
                        turn_lnd(b, head)
                    if back and k == 12:
                        if front:
                            pe.wait_ge(xin_done, b + 2)
                        pe.wait_ge(up_done, FC * (b - 1) + 2)
                        up_matmul(b, *UP_SLOT[k])
                    if head and k == 13:
                        pe.wait_ge(xhat_done, b + 3)
                        if front:
                            pe.wait_ge(lndT_done if first_front else xin_done, b + 2)
                        let_pass(pe)
                        for j in range(JB):
                            last = nc.tensor.transpose(side[0:IN, 0, j * P:(j + 1) * P], xhat[:, j, :], ident[:, :])
                        last.then_inc(xhatT_mm, 1)
                    if head and k == 15:
                        pe.wait_ge(xhatT_done, b + 3)
                        let_pass(pe)
                        nc.tensor.matmul(side[0:H, 0, :], w1g[:, :], xhatT[:, :], start=True, stop=True).then_inc(hid_mm, 1)
                    if back and k in (14, 15, 16):
                        pe.wait_ge(up_done, FC * (b - 1) + k - 11)
                        up_matmul(b, *UP_SLOT[k])
                    if head and k == 17:
                        pe.wait_ge(hid_done, b + 3)
                        if back:
                            pe.wait_ge(up_done, FC * b)
                        for j in range(JB):
                            last = nc.tensor.matmul(side[:, j // 2, (j % 2) * D:(j % 2 + 1) * D], hidT[:, j * P:(j + 1) * P],
                                                    w2_sb[:, :], start=True, stop=True)
                        last.then_inc(h0_mm, 1)
                    if front and k == 19 and not first_front:
                        turn_lnd(b, head)
                    if back and k == 21:
                        pe.wait_ge(hq_done, 4 * b)
                        if front:
                            pe.wait_ge(lndT_done, b + 2)
                        for j in range(JB):
                            for c in range(FC):
                                last = nc.tensor.matmul(side[:, j // 2, (j % 2) * D:(j % 2 + 1) * D], hq[:, c, j * P:(j + 1) * P],
                                                        wq2[:, c, :], start=(c == 0), stop=(c == FC - 1))
                        last.then_inc(down_mm, 1)
                    if k % TG == 1:
                        weigh_ahead(b, k + 2, front, main)

            passes(pe, body)


_OUT_SHAPE = (16, 512, 192)


def kernel(**inputs):
    import numpy as _np
    import concourse.bacc as _bacc
    from concourse import mybir as _mybir
    from concourse.bass_utils import run_bass_kernel_spmd as _run

    t = {k[len("L0_tok_"):]: _np.asarray(v) for k, v in inputs.items() if k.startswith("L0_tok_")}
    a = {k[len("L0_attn_"):]: _np.asarray(v) for k, v in inputs.items() if k.startswith("L0_attn_")}
    f = {k[len("L0_ffn_"):]: _np.asarray(v) for k, v in inputs.items() if k.startswith("L0_ffn_")}
    row = lambda v: v.reshape(1, -1)
    col = lambda v: v.reshape(-1, 1)
    lanes = lambda v: v.reshape(-1, 128).T
    A_log = a["A_log"]
    order = [0, 2, 1] + list(range(3, t["W1"].shape[0]))
    arrays = dict(
        tok_ids=lanes(_np.asarray(inputs["x"])), var_ids=_np.asarray(inputs["itok_BS_0_511"]),
        tok_table=_np.stack([t["token_" + n] for n in ("has_int", "log_norm", "signed_norm", "is_zero", "is_one", "is_pow2")], 1),
        fam_onehot=t["var_family_onehot"],
        var_cols=_np.stack([t["var_" + n] for n in ("outer_norm", "inner_norm", "has_outer", "has_inner")], 1),
        var_int=_np.stack([t["var_family_id"], t["var_group_id"]], 1),
        ln_gamma=col(t["ln_gamma"][order]), ln_beta=col(t["ln_beta"][order]), W1=t["W1"][order], b1=col(t["b1"]), W2=t["W2"], b2=row(t["b2"]),
        tok_scale=t["scale"].reshape(1, 1),
        A_log_lo=A_log[:128], A_log_hi=_np.concatenate([A_log[128:, 0::2], A_log[128:, 1::2]], 0),
        D_param=row(a["D_param"]), W_bc=a["W_bc"], W_dt=a["W_dt"], W_dtp=a["W_dtp"], b_dt=row(a["b_dt"]),
        rms_scale=row(a["rms_scale"]),
        ffn_w1T=f["w1"].T, ffn_b1=lanes(f["b1"]), alpha_w1_col=lanes(f["alpha_w1"]), alpha_w1_row=row(f["alpha_w1"]),
        alpha_a1=row(f["alpha_a1"]), ffn_w2T=f["w2"].T, ffn_b2=row(f["b2"]), alpha_w2=row(f["alpha_w2"]),
        alpha_a2=row(f["alpha_a2"]))
    nc = _bacc.Bacc("TRN2", target_bir_lowering=False, num_devices=1)
    fed, args = {}, {}
    for name, v in arrays.items():
        fed[f"in_{name}"] = _np.ascontiguousarray(v)
        args[name] = nc.dram_tensor(f"in_{name}", v.shape, _mybir.dt.from_np(v.dtype), kind="ExternalInput").ap()
    args["out"] = nc.dram_tensor("out_h", _OUT_SHAPE, _mybir.dt.float32, kind="ExternalOutput").ap()
    lm_tower_kernel(nc, **args)
    r = _run(nc, [fed], core_ids=[0])
    return r.results[0]["out_h"]
```
